# Optimizing a Trainium2 kernel written in Bass

```python
import numpy as np
import jax
import jax.numpy as jnp

def _softmax(x, axis=-1):
    return jax.nn.softmax(x, axis=axis)

def _gelu(x):
    return jax.nn.gelu(x, approximate=True)

def _silu(x):
    return jax.nn.silu(x)

def _sigmoid(x):
    return jax.nn.sigmoid(x)

def _layernorm(x, axis=-1, eps=1e-05):
    m = jnp.mean(x, axis=axis, keepdims=True)
    v = jnp.var(x, axis=axis, keepdims=True)
    return (x - m) / jnp.sqrt(v + eps)

def _scatter_add(tgt, idx, src, axis=0):
    return tgt.at[idx].add(src)

def _segment_sum(src, seg, n):
    return jax.ops.segment_sum(src, seg, n)
kernel_name = 'mk_xattn_seq_d1_seqx_r2_80a393'

def setup_inputs(seed: int=0):
    np.random.seed(seed)
    _w = jnp.asarray

    def _rec_inputs():
        import jax
        import jax.numpy as jnp
        _rk = jax.random.key(seed)
        x = -0.0002928 + 1 * jax.random.normal(jax.random.fold_in(_rk, 1), (16, 512, 512), jnp.float32)
        _lenS = 512 - jax.random.randint(jax.random.fold_in(_rk, 7), (16,), 0, max(1, 512 // 4) + 1, jnp.int32)
        _lenS2 = 512 - jax.random.randint(jax.random.fold_in(_rk, 8), (16,), 0, max(1, 512 // 4) + 1, jnp.int32)
        _ctx_1024P = jax.random.normal(jax.random.fold_in(_rk, 11), (16, 16, 512), jnp.float32)
        _ctx_1024c = jax.random.dirichlet(jax.random.fold_in(_rk, 511), 0.3 * jnp.ones((16,), jnp.float32), (16, 512))
        _ctx_1024t = jnp.einsum('bsk,bkd->bsd', _ctx_1024c, _ctx_1024P)
        _ctx_1024t = _ctx_1024t * jax.lax.rsqrt(jnp.mean(jnp.square(_ctx_1024t)) + 1e-12) * 0.953939
        ctx_1024 = -1.39393e-06 + 0.999914 * (_ctx_1024t + 0.3 * jax.random.normal(jax.random.fold_in(_rk, 611), (16, 512, 512), jnp.float32))
        return (x, ctx_1024)
    x, ctx_1024 = _rec_inputs()

    def _L0_xattn_setup():
        import jax, jax.numpy as jnp
        import numpy as np
        D_MODEL = 512
        N_HEADS = 16
        D_K = D_MODEL // N_HEADS
        D_FF = 2048
        B, S = (2, 1024)
        LN_EPS = 1e-05
        NEG_INF = -1e+30

        def layer_norm(x, g, b):
            mu = jnp.mean(x, axis=-1, keepdims=True)
            var = jnp.mean(jnp.square(x - mu), axis=-1, keepdims=True)
            return (x - mu) * jax.lax.rsqrt(var + LN_EPS) * g + b
        key = jax.random.key(seed)
        ks = jax.random.split(key, 16)
        sd = 0.02
        inp = {'query': jax.random.normal(ks[0], (B, S, D_MODEL), jnp.float32), 'key': jax.random.normal(ks[1], (B, S, D_MODEL), jnp.float32), 'values': jax.random.normal(ks[2], (B, S, D_MODEL), jnp.float32), 'Wq': jax.random.normal(ks[3], (D_MODEL, D_MODEL), jnp.float32) * sd, 'bq': jnp.zeros((D_MODEL,), jnp.float32), 'Wk': jax.random.normal(ks[4], (D_MODEL, D_MODEL), jnp.float32) * sd, 'bk': jnp.zeros((D_MODEL,), jnp.float32), 'Wv': jax.random.normal(ks[5], (D_MODEL, D_MODEL), jnp.float32) * sd, 'bv': jnp.zeros((D_MODEL,), jnp.float32), 'Wo': jax.random.normal(ks[6], (D_MODEL, D_MODEL), jnp.float32) * sd, 'bo': jnp.zeros((D_MODEL,), jnp.float32), 'ln1_g': jnp.ones((D_MODEL,), jnp.float32), 'ln1_b': jnp.zeros((D_MODEL,), jnp.float32), 'W1': jax.random.normal(ks[7], (D_MODEL, D_FF), jnp.float32) * sd, 'b1': jnp.zeros((D_FF,), jnp.float32), 'W2': jax.random.normal(ks[8], (D_FF, D_MODEL), jnp.float32) * sd, 'b2': jnp.zeros((D_MODEL,), jnp.float32), 'ln2_g': jnp.ones((D_MODEL,), jnp.float32), 'ln2_b': jnp.zeros((D_MODEL,), jnp.float32), 'mask': 0}
        return inp
    _L0_xattn_all = _L0_xattn_setup()
    _L0_xattn_in = {k: v for k, v in _L0_xattn_all.items() if k in ('Wq', 'bq', 'Wk', 'bk', 'Wv', 'bv', 'Wo', 'bo', 'ln1_g', 'ln1_b', 'W1', 'b1', 'W2', 'b2', 'ln2_g', 'ln2_b')}
    del _L0_xattn_all
    return {'x': x, 'ctx_1024': ctx_1024, 'L0_xattn_Wq': _L0_xattn_in['Wq'], 'L0_xattn_bq': _L0_xattn_in['bq'], 'L0_xattn_Wk': _L0_xattn_in['Wk'], 'L0_xattn_bk': _L0_xattn_in['bk'], 'L0_xattn_Wv': _L0_xattn_in['Wv'], 'L0_xattn_bv': _L0_xattn_in['bv'], 'L0_xattn_Wo': _L0_xattn_in['Wo'], 'L0_xattn_bo': _L0_xattn_in['bo'], 'L0_xattn_ln1_g': _L0_xattn_in['ln1_g'], 'L0_xattn_ln1_b': _L0_xattn_in['ln1_b'], 'L0_xattn_W1': _L0_xattn_in['W1'], 'L0_xattn_b1': _L0_xattn_in['b1'], 'L0_xattn_W2': _L0_xattn_in['W2'], 'L0_xattn_b2': _L0_xattn_in['b2'], 'L0_xattn_ln2_g': _L0_xattn_in['ln2_g'], 'L0_xattn_ln2_b': _L0_xattn_in['ln2_b']}

def reference(x, ctx_1024, L0_xattn_Wq, L0_xattn_bq, L0_xattn_Wk, L0_xattn_bk, L0_xattn_Wv, L0_xattn_bv, L0_xattn_Wo, L0_xattn_bo, L0_xattn_ln1_g, L0_xattn_ln1_b, L0_xattn_W1, L0_xattn_b1, L0_xattn_W2, L0_xattn_b2, L0_xattn_ln2_g, L0_xattn_ln2_b):
    import jax
    import jax.numpy as jnp

    def _L0_xattn_ref(query, key, values, Wq, bq, Wk, bk, Wv, bv, Wo, bo, ln1_g, ln1_b, W1, b1, W2, b2, ln2_g, ln2_b, mask):
        import jax, jax.numpy as jnp
        import numpy as np
        D_MODEL = 512
        N_HEADS = 16
        D_K = D_MODEL // N_HEADS
        D_FF = 2048
        B, S = (2, 1024)
        LN_EPS = 1e-05
        NEG_INF = -1e+30

        def layer_norm(x, g, b):
            mu = jnp.mean(x, axis=-1, keepdims=True)
            var = jnp.mean(jnp.square(x - mu), axis=-1, keepdims=True)
            return (x - mu) * jax.lax.rsqrt(var + LN_EPS) * g + b
        b, s, d = query.shape
        q = (query @ Wq + bq).reshape(b, s, N_HEADS, D_K).transpose(0, 2, 1, 3)
        k = (key @ Wk + bk).reshape(b, s, N_HEADS, D_K).transpose(0, 2, 1, 3)
        v = (values @ Wv + bv).reshape(b, s, N_HEADS, D_K).transpose(0, 2, 1, 3)
        scores = jnp.einsum('bhqd,bhkd->bhqk', q, k) / jnp.sqrt(jnp.float32(D_K))
        i = jnp.arange(s)[:, None]
        j = jnp.arange(s)[None, :]
        allowed = j < i + mask
        scores = jnp.where(allowed, scores, NEG_INF)
        attn = jax.nn.softmax(scores, axis=-1)
        if mask == 0:
            attn = attn.at[:, :, 0, :].set(0.0)
        ctx = jnp.einsum('bhqk,bhkd->bhqd', attn, v)
        ctx = ctx.transpose(0, 2, 1, 3).reshape(b, s, d)
        attn_out = ctx @ Wo + bo
        x = layer_norm(query + attn_out, ln1_g, ln1_b)
        ffn = jax.nn.relu(x @ W1 + b1) @ W2 + b2
        out = layer_norm(x + ffn, ln2_g, ln2_b)
        return out
    x = _L0_xattn_ref(x, ctx_1024, ctx_1024, L0_xattn_Wq, L0_xattn_bq, L0_xattn_Wk, L0_xattn_bk, L0_xattn_Wv, L0_xattn_bv, L0_xattn_Wo, L0_xattn_bo, L0_xattn_ln1_g, L0_xattn_ln1_b, L0_xattn_W1, L0_xattn_b1, L0_xattn_W2, L0_xattn_b2, L0_xattn_ln2_g, L0_xattn_ln2_b, 0)
    return x

_drawn_inputs = setup_inputs


def setup_inputs(seed=0):
    import zlib

    import numpy as np

    out = dict(_drawn_inputs(seed))
    spreads = {'L0_xattn_bq': (0.0, 0.8),
     'L0_xattn_bk': (0.0, 0.8),
     'L0_xattn_bv': (0.0, 0.1),
     'L0_xattn_bo': (0.0, 0.1),
     'L0_xattn_ln1_g': (1.0, 0.2),
     'L0_xattn_ln1_b': (0.0, 0.1),
     'L0_xattn_b1': (0.0, 0.1),
     'L0_xattn_b2': (0.0, 0.1),
     'L0_xattn_ln2_g': (1.0, 0.2),
     'L0_xattn_ln2_b': (0.0, 0.1)}
    factors = {'L0_xattn_Wq': 7.326, 'L0_xattn_Wk': 7.108}
    for name, (base, spread) in spreads.items():
        noise = np.random.default_rng([zlib.crc32(name.encode()), seed]).standard_normal(out[name].shape)
        drawn = base * np.exp(spread * noise) if base else spread * noise
        out[name] = jnp.asarray(drawn.astype(out[name].dtype))
    for name, factor in factors.items():
        out[name] = (out[name] * factor).astype(out[name].dtype)
    return out
```

```python
import numpy as np

import concourse.bass as bass
from concourse import mybir
from contextlib import ExitStack

F32 = mybir.dt.float32
F32R = mybir.dt.float32r
BF16 = mybir.dt.bfloat16
F16 = mybir.dt.float16
ALU = mybir.AluOpType
ACT = mybir.ActivationFunctionType
AX_X = mybir.AxisListType.X

P = 128
HEADS = 16
MASKED = -1e30
LN_EPS = 1e-5
PROB_BITS = 10
BACK = 2


class Item:

    def __init__(self, n, parity):
        self.n, self.parity = n, parity


def due(window, slot, slots, items, first, span=1):
    n, parity = window
    for back in range(BACK + 1):
        k = slot + slots * back - first
        if 0 <= k < span:
            at = n - back if back else n
            if not isinstance(at, int) or 0 <= at < items:
                yield Item(at, (parity - back) % 2), k


def wait_for(eng, sem, per, item, c):
    if isinstance(item.n, int):
        if per * item.n + c > 0:
            eng.wait_ge(sem, per * item.n + c)
    else:
        eng.wait_ge(sem, item.n * per + c if c else item.n * per)


def wait_for_all(eng, *waits):
    values = []
    for sem, per, item, c in waits:
        if isinstance(item.n, int):
            values.append(per * item.n + c)
        else:
            values.append(eng.snap(eng.to_reg(item.n * per + c)))
    for (sem, _, item, _), value in zip(waits, values):
        if not isinstance(item.n, int) or value > 0:
            eng.wait_ge(sem, value)


def run_windows(eng, items, emit, peeled=BACK):
    for w in range(peeled):
        emit((w, w % 2))
    with eng.Fori(0, (items - peeled) // 2) as pair:
        for parity in range(2):
            emit((pair * 2 + (peeled + parity), parity))
    for w in range(items, items + BACK):
        emit((w, w % 2))


def attention(nc, xT, cT, weights, biases, bv, ctx_rows):
    B, D, S = xT.shape
    KT = D // P
    GROUPS = HEADS // 4
    HD = D // HEADS
    QT = S // P
    VW = 3 * HD + 2
    SLOTS = 12 * GROUPS
    SCALE = float(HD) ** -0.5
    PROB_BIAS = PROB_BITS * float(np.log(2.0))
    assert D == S == 512 and HD == 32 and B % 2 == 0 and B > BACK

    CTX_LOAD = 0
    CTX_SPLIT = 26
    X_LOAD = 28
    X_SPLIT = 34
    LIN = 32
    OUT = LIN + 4
    MAX_AT = LIN + 25
    ROW_AT = MAX_AT + 14
    ST_AT = ROW_AT + 6
    PV_AT = ST_AT + 4
    UNITS = [("v", 0), ("v", 1), ("k", 0), ("q", 0), ("v", 2), ("k", 1), ("q", 1), ("v", 3),
             ("k", 2), ("q", 2), ("k", 3), ("q", 3)]
    KQ_INDEX = {u: n for n, u in enumerate(u for u in UNITS if u[0] != "v")}
    GROUP_READY = {t: OUT + 4 * UNITS.index(("q", t)) + 1 for t in range(GROUPS)}
    MAX_UNITS = {0: (0, (0, 1, 2, 3)), 1: (1, (0, 1)), 3: (1, (2, 3)),
                 4: (2, (0,)), 5: (2, (1,)), 6: (2, (2,)), 7: (2, (3,)),
                 8: (3, (0,)), 9: (3, (1,)), 10: (3, (2,)), 11: (3, (3,))}
    MAX_NUMBER = {s: n for n, s in enumerate(MAX_UNITS)}
    NMAX = len(MAX_UNITS)
    ST_UNITS = [((0, 0),), ((1, 0), (3, 3 * P)), ((2, 0),)]
    ST_WIDTH = [4 * P, 4 * P, 2 * P]
    NW = 3 * KT
    NCHUNK = 2 * KT
    RAW = 4

    with ExitStack() as stack:
        def sb(name, shape, dt):
            return stack.enter_context(nc.sbuf_tensor(name, shape, dt))

        def sem(name):
            return stack.enter_context(nc.semaphore(name))

        W = {w: sb(f"w{w}", [P, 2, KT, D], F32R) for w in "vkq"}
        acts = {"c": sb("ctxT", [P, 2, KT, S], F32R), "x": sb("xT", [P, 2, KT, S], F32R)}
        heads = sb("heads", [P, GROUPS, 2, 4, S], F32R)
        raw = sb("raw", [P, RAW, D], F32)
        stage = sb("stage", [P, 2, 2, 2, S], F32R)
        vf = sb("vf", [P, D], F32)
        V = sb("V", [P, 2, QT, HEADS, VW], BF16)
        probs = sb("probs", [P, 3, S], F32)
        prob_hi = sb("prob_hi", [P, 4, S], F16)
        prob_lo = sb("prob_lo", [P, 4, S], F16)
        maxima = sb("maxima", [P, 2, QT, 4], F32)
        negmax = sb("negmax", [P, QT, 4], F32)
        negmax_parts = sb("negmax_parts", [P, 2, QT, 2, 4], F32)
        rows = sb("rows", [8, 2, S], F32R)
        osum = sb("osum", [P, QT, HD], F32)
        den = sb("den", [P, QT], F32)
        rden = sb("rden", [P, QT], F32)
        onorm = sb("onorm", [P, 2, QT, 4, HD], F32)
        bias = {"k": sb("bk", [P, GROUPS], F32), "q": sb("bq", [P, GROUPS], F32)}
        bvb = sb("bvb", [P, D], F32)
        ident = sb("ident", [P, P], F32)
        identb = sb("identb", [P, P], BF16)
        zeros = sb("zeros", [P, P], BF16)
        mask_q = sb("mask_q", [P, 4, P], BF16)
        mask_k = sb("mask_k", [P, P], BF16)

        lin_ps = stack.enter_context(nc.psum_tensor("lin_ps", [P, 2, 512], F32))
        max_ps = stack.enter_context(nc.psum_tensor("max_ps", [P, 2, 512], F32))
        st_ps = stack.enter_context(nc.psum_tensor("st_ps", [P, 2, 512], F32))
        o_ps = stack.enter_context(nc.psum_tensor("o_ps", [P, 2, 512], F32))

        consts = sem("consts")
        const_loaded = sem("const_loaded")
        raw_loaded = [sem(f"raw_loaded{i}") for i in range(RAW)]
        hi_done = sem("hi_done")
        lo_done = sem("lo_done")
        lin_step = sem("lin_step")
        kq_hi = sem("kq_hi")
        lin_out = sem("lin_out")
        v_hi = sem("v_hi")
        v_rest = sem("v_rest")
        v_mid = sem("v_mid")
        v_lo = sem("v_lo")
        heads_loaded = [sem(f"heads_loaded{t}") for t in range(GROUPS)]
        max_done = sem("max_done")
        max_read = sem("max_read")
        neg_step = sem("neg_step")
        parts_ready = sem("parts_ready")
        rows_done = sem("rows_done")
        rows_out = sem("rows_out")
        rows_loaded = [sem(f"rows_loaded{i}") for i in range(2)]
        st_done = sem("st_done")
        exp_done = sem("exp_done")
        pl_done = sem("pl_done")
        pv_done = sem("pv_done")
        o_step = sem("o_step")
        o_read = sem("o_read")
        o_out = sem("o_out")
        stored = [sem(f"stored{i}") for i in range(2)]

        def chunk_of(kind, item, j):
            return NW + j + (KT if kind == "x" else 0)

        block = stack.enter_context(nc.Block())

        @block.sync
        def _(sp):
            def load(dst_n, src, item, c):
                wait_for_all(sp, (lo_done, NCHUNK, item, c - RAW + 1))
                sp.dma_start(raw[:, dst_n, :], src).then_inc(raw_loaded[dst_n], 16)

            start = Item(0, 0)
            for n, w in enumerate("vkq"):
                view = weights[w].rearrange("(k p) n -> k p n", p=P)
                for j in range(KT):
                    c = n * KT + j
                    load(c % RAW, view[j], start, c)
            for w in "kq":
                sp.dma_start(bias[w][:, :], biases[w]).then_inc(const_loaded, 16)
            sp.dma_start(bvb[:, :], bv.rearrange("(a n) -> a n", a=1).to_broadcast([P, D])).then_inc(const_loaded, 16)

            def source(a, item, j):
                if isinstance(item.n, int):
                    return a[item.n, j * P:(j + 1) * P, :]
                return a[bass.ds(sp.snap(item.n), 1), j * P:(j + 1) * P, :].rearrange("a p s -> (a p) s")

            def emit(window):
                for s in range(SLOTS):
                    for j in range(KT):
                        for item, _ in due(window, s, SLOTS, B, CTX_LOAD + 2 * j):
                            load((NW + j) % RAW, source(cT, item, j), item, NW + j)
                        for item, _ in due(window, s, SLOTS, B, X_LOAD + 2 * j):
                            load((NW + KT + j) % RAW, source(xT, item, j), item, NW + KT + j)
                    for t in range(GROUPS):
                        for item, _ in due(window, s, SLOTS, B, GROUP_READY[t]):
                            wait_for_all(sp, (lin_out, len(UNITS), item, UNITS.index(("q", t)) + 1),
                                         (st_done, SLOTS, item, 12 * t + 12 - SLOTS))
                            for part in range(3):
                                for i in range(4):
                                    four = stage[32 * i:32 * i + 32, t % 2, :, :, :].rearrange("p a b n -> p (a b) n")
                                    pick = (four[:, 0:3:2, :], four[:, 1:3, :], four[:, 0:4:3, :])[part]
                                    sp.dma_start(heads[32 * part:32 * part + 32, t, :, i, :].bitcast(F32),
                                                 pick.bitcast(F32)).then_inc(heads_loaded[t], 16)
                    for t in range(GROUPS):
                        for item, _ in due(window, s, SLOTS, B, ROW_AT + 12 * t + 1):
                            wait_for_all(sp, (rows_out, GROUPS, item, t + 1))
                            for part in range(2):
                                sp.dma_start(heads[96 + part:97 + part, t, 0, :, :].bitcast(F32),
                                             rows[4 * part:4 * part + 4, t % 2, :].bitcast(F32)
                                             ).then_inc(rows_loaded[t % 2], 16)
                    for t in range(GROUPS):
                        for item, _ in due(window, s, SLOTS, B, PV_AT + 12 * t + 14):
                            f = t * P
                            if isinstance(item.n, int):
                                dst = ctx_rows[item.n * S:(item.n + 1) * S, f:f + P]
                            else:
                                dst = ctx_rows[bass.ds(sp.snap(item.n * S), S), f:f + P]
                            wait_for_all(sp, (o_out, HEADS, item, 4 * t + 4))
                            sp.dma_start(dst.rearrange("(q p) n -> p q n", p=P),
                                         onorm[:, t % 2, :, :, :].rearrange("p q h d -> p q (h d)")
                                         ).then_inc(stored[t % 2], 16)

            run_windows(sp, B, emit)
            for i in range(2):
                sp.wait_ge(stored[i], 16 * B * GROUPS // 2)

        @block.gpsimd
        def _(pool):
            pool.memset(ident[:, :], 0.0).then_inc(consts, 1)
            pool.memset(zeros[:, :], 0.0).then_inc(consts, 1)
            pool.wait_ge(consts, 2)
            pool.memset(heads[96:98, :, 1, :, :].bitcast(F32), 1.0).then_inc(consts, 1)
            pool.wait_ge(consts, 3)
            pool.memset(V[:, :, :, :, 3 * HD:VW], 1.0).then_inc(consts, 1)
            pool.wait_ge(consts, 4)
            pool.affine_select(out=ident[:, :], in_=ident[:, :], compare_op=ALU.not_equal, fill=1.0,
                               base=0, pattern=[[-1, P]], channel_multiplier=1).then_inc(consts, 1)
            pool.affine_select(out=identb[:, :], in_=zeros[:, :], compare_op=ALU.not_equal, fill=1.0,
                               base=0, pattern=[[-1, P]], channel_multiplier=1).then_inc(consts, 1)
            for i in range(4):
                pool.affine_select(out=mask_q[:, i, :], in_=zeros[:, :], compare_op=ALU.is_gt, fill=MASKED,
                                   base=0, pattern=[[-1, P]], channel_multiplier=1).then_inc(consts, 1)
            pool.affine_select(out=mask_k[:, :], in_=zeros[:, :], compare_op=ALU.is_gt, fill=MASKED,
                               base=0, pattern=[[1, P]], channel_multiplier=-1).then_inc(consts, 1)

            def emit(window):
                for s in range(SLOTS):
                    for item, k in due(window, s, SLOTS, B, ST_AT, SLOTS):
                        w = ST_WIDTH[k % 3]
                        wait_for(pool, exp_done, SLOTS, item, k + 1)
                        wait_for(pool, pv_done, SLOTS, item, k + 1 - 4)
                        pool.tensor_tensor(prob_lo[:, k % 4, 0:w], probs[:, k % 3, 0:w],
                                           prob_hi[:, k % 4, 0:w], ALU.subtract).then_inc(pl_done, 1)

            run_windows(pool, B, emit)

        @block.scalar
        def _(act):
            def split(item, c, dst):
                wait_for(act, raw_loaded[c % RAW], 16 * NCHUNK // RAW, item, 16 * (c // RAW + 1))
                act.activation(dst, raw[:, c % RAW, :], ACT.Copy).then_inc(hi_done, 1)

            start = Item(0, 0)
            for n, w in enumerate("vkq"):
                for j in range(KT):
                    split(start, n * KT + j, W[w][:, 0, j, :])
            act.wait_ge(const_loaded, 48)

            def emit(window):
                for s in range(SLOTS):
                    for t in range(GROUPS):
                        for item, _ in due(window, s, SLOTS, B, ROW_AT + 12 * t + 1):
                            wait_for(act, rows_done, GROUPS, item, t + 1)
                            wait_for(act, rows_loaded[t % 2], 64, item, 32 * (t // 2))
                            act.activation(rows[:, t % 2, :], max_ps[0:8, (ROW_AT + 12 * t) % 2, :], ACT.Copy
                                           ).then_inc(rows_out, 1)
                    for n, (kind, t) in enumerate(UNITS):
                        if kind == "v":
                            for item, _ in due(window, s, SLOTS, B, OUT + 4 * n + 1):
                                wait_for(act, lin_out, len(UNITS), item, n + 1)
                                wait_for(act, pv_done, SLOTS, item, -SLOTS)
                                act.activation(V[:, item.parity, t, :, HD:2 * HD],
                                               vf[:, :].rearrange("p (h d) -> p h d", d=HD), ACT.Copy
                                               ).then_inc(v_hi, 1)
                            for item, _ in due(window, s, SLOTS, B, OUT + 4 * n + 3):
                                wait_for(act, v_rest, QT, item, t + 1)
                                act.activation(V[:, item.parity, t, :, 2 * HD:3 * HD],
                                               vf[:, :].rearrange("p (h d) -> p h d", d=HD), ACT.Copy
                                               ).then_inc(v_mid, 1)
                        else:
                            for item, _ in due(window, s, SLOTS, B, OUT + 4 * n):
                                wait_for(act, lin_step, SLOTS, item, 4 * n + 4)
                                wait_for(act, heads_loaded[(t - 2) % GROUPS], 192, item, 192 if t > 1 else 0)
                                act.activation(stage[:, t % 2, "qk".index(kind), 0, :], lin_ps[:, n % 2, :], ACT.Identity,
                                               bias=bias[kind][:, t:t + 1]).then_inc(kq_hi, 1)
                    for j in range(KT):
                        for item, _ in due(window, s, SLOTS, B, CTX_SPLIT + 2 * j):
                            wait_for(act, lin_step, SLOTS, item, 4 * UNITS.index(("k", 3)) + j + 1 - SLOTS)
                            split(item, NW + j, acts["c"][:, 0, j, :])
                        for item, _ in due(window, s, SLOTS, B, X_SPLIT + 2 * j):
                            wait_for(act, lin_step, SLOTS, item, 4 * UNITS.index(("q", 3)) + j + 1 - SLOTS)
                            split(item, NW + KT + j, acts["x"][:, 0, j, :])
                    for item, k in due(window, s, SLOTS, B, ST_AT, SLOTS):
                        w = ST_WIDTH[k % 3]
                        wait_for(act, st_done, SLOTS, item, k + 1)
                        wait_for(act, pl_done, SLOTS, item, k + 1 - 3)
                        wait_for(act, pv_done, SLOTS, item, k + 1 - 4)
                        act.activation(probs[:, k % 3, 0:w], st_ps[:, k % 2, 0:w], ACT.Exp, bias=PROB_BIAS,
                                       scale=SCALE)
                        act.activation(prob_hi[:, k % 4, 0:w], st_ps[:, k % 2, 0:w], ACT.Exp, bias=PROB_BIAS,
                                       scale=SCALE
                                       ).then_inc(exp_done, 1)

            run_windows(act, B, emit)

        @block.vector
        def _(dve):
            def split(item, c, hi, lo):
                wait_for(dve, hi_done, NCHUNK, item, c + 1)
                dve.tensor_tensor(lo, raw[:, c % RAW, :], hi, ALU.subtract).then_inc(lo_done, 1)

            start = Item(0, 0)
            for n, w in enumerate("vkq"):
                for j in range(KT):
                    split(start, n * KT + j, W[w][:, 0, j, :], W[w][:, 1, j, :])
            dve.wait_ge(const_loaded, 48)

            def emit(window):
                for s in range(SLOTS):
                    for n, (kind, t) in enumerate(UNITS):
                        if kind == "v":
                            for item, _ in due(window, s, SLOTS, B, OUT + 4 * n):
                                wait_for(dve, lin_step, SLOTS, item, 4 * n + 4)
                                wait_for(dve, v_lo, QT, item, t)
                                dve.tensor_tensor(vf[:, :], lin_ps[:, n % 2, :], bvb[:, :], ALU.add
                                                  ).then_inc(lin_out, 1)
                            vr = vf[:, :].rearrange("p (h d) -> p h d", d=HD)
                            for item, _ in due(window, s, SLOTS, B, OUT + 4 * n + 2):
                                wait_for(dve, v_hi, QT, item, t + 1)
                                dve.tensor_tensor(vr, vr, V[:, item.parity, t, :, HD:2 * HD], ALU.subtract
                                                  ).then_inc(v_rest, 1)
                            for item, _ in due(window, s, SLOTS, B, OUT + 4 * n + 4):
                                wait_for(dve, v_mid, QT, item, t + 1)
                                dve.tensor_tensor(V[:, item.parity, t, :, 0:HD], vr,
                                                  V[:, item.parity, t, :, 2 * HD:3 * HD], ALU.subtract
                                                  ).then_inc(v_lo, 1)
                        else:
                            qk = "qk".index(kind)
                            for item, _ in due(window, s, SLOTS, B, OUT + 4 * n + 1):
                                wait_for(dve, kq_hi, len(KQ_INDEX), item, KQ_INDEX[kind, t] + 1)
                                dve.scalar_tensor_tensor(out=stage[:, t % 2, qk, 1, :], in0=lin_ps[:, n % 2, :],
                                                         scalar=bias[kind][:, t:t + 1], in1=stage[:, t % 2, qk, 0, :],
                                                         op0=ALU.add, op1=ALU.subtract).then_inc(lin_out, 1)
                    for j in range(KT):
                        for item, _ in due(window, s, SLOTS, B, CTX_SPLIT + 2 * j + 1):
                            split(item, NW + j, acts["c"][:, 0, j, :], acts["c"][:, 1, j, :])
                        for item, _ in due(window, s, SLOTS, B, X_SPLIT + 2 * j + 1):
                            split(item, NW + KT + j, acts["x"][:, 0, j, :], acts["x"][:, 1, j, :])
                    for h in range(HEADS):
                        t, i = h // 4, h % 4
                        o = o_ps[:, h % 2, 0:QT * VW].rearrange("p (q w) -> p q w", w=VW)
                        for item, _ in due(window, s, SLOTS, B, PV_AT + 3 * h + 3):
                            wait_for(dve, pv_done, SLOTS, item, 3 * h + 3)
                            wait_for(dve, o_out, HEADS, item, h)
                            dve.tensor_scalar(den[:, :], o[:, :, 3 * HD], 1e-30, None, ALU.max).then_inc(o_step, 1)
                            dve.tensor_reduce(osum[:, :, :],
                                              o[:, :, 0:3 * HD].rearrange("p q (c d) -> p q d c", c=3),
                                              AX_X, ALU.add).then_inc(o_read, 1)
                            wait_for(dve, o_step, 2 * HEADS, item, 2 * h + 1)
                            dve.reciprocal(rden[:, :], den[:, :]).then_inc(o_step, 1)
                        for item, _ in due(window, s, SLOTS, B, PV_AT + 3 * h + 4):
                            wait_for(dve, o_read, HEADS, item, h + 1)
                            wait_for(dve, o_step, 2 * HEADS, item, 2 * h + 2)
                            if i == 0:
                                wait_for(dve, stored[t % 2], 32, item, 16 * (t // 2))
                            dve.tensor_tensor(onorm[:, t % 2, :, i, :], osum[:, :, :],
                                              rden[:, :].unsqueeze(2).to_broadcast([P, QT, HD]), ALU.mult
                                              ).then_inc(o_out, 1)
                    for t in range(GROUPS):
                        for item, _ in due(window, s, SLOTS, B, MAX_AT + 12 * t + 12):
                            wait_for(dve, max_read, NMAX * GROUPS, item, NMAX * (t + 1))
                            wait_for(dve, parts_ready, GROUPS, item, t)
                            dve.tensor_scalar(negmax[:, :, :], maxima[:, t % 2, :, :], -1e28, -1.0, ALU.max, ALU.mult
                                              ).then_inc(neg_step, 1)
                            wait_for(dve, neg_step, 2 * GROUPS, item, 2 * t + 1)
                            wait_for(dve, rows_done, GROUPS, item, t - 1)
                            hi = negmax_parts[:, t % 2, :, 0, :]
                            dve.tensor_copy(hi.bitcast(F32R), negmax[:, :, :]).then_inc(neg_step, 1)
                            wait_for(dve, neg_step, 2 * GROUPS, item, 2 * t + 2)
                            dve.tensor_tensor(negmax_parts[:, t % 2, :, 1, :].bitcast(F32R), negmax[:, :, :], hi,
                                              ALU.subtract).then_inc(parts_ready, 1)
                    for t in range(GROUPS):
                        for item, k in due(window, s, SLOTS, B, MAX_AT + 12 * t, 12):
                            if k in MAX_UNITS:
                                q, hs = MAX_UNITS[k]
                                n = NMAX * t + MAX_NUMBER[k]
                                wait_for(dve, max_done, NMAX * GROUPS, item, n + 1)
                                if k == 0:
                                    wait_for(dve, parts_ready, GROUPS, item, t - 1)
                                bank = max_ps[:, (MAX_AT + 12 * t + k) % 2, 0:len(hs) * P * (q + 1)]
                                dve.tensor_reduce(maxima[:, t % 2, q, hs[0]:hs[0] + len(hs)],
                                                  bank.rearrange("p (h n) -> p h n", h=len(hs)), AX_X, ALU.max
                                                  ).then_inc(max_read, 1)

            run_windows(dve, B, emit)

        @block.tensor
        def _(pe):
            pe.wait_ge(consts, 11)

            def scores_for_max(item, t, k):
                q, hs = MAX_UNITS[k]
                bank = (MAX_AT + 12 * t + k) % 2
                n = NMAX * t + MAX_NUMBER[k]
                if k == 0:
                    wait_for(pe, heads_loaded[t], 192, item, 192)
                if k == 4:
                    wait_for(pe, rows_out, GROUPS, item, t)
                else:
                    wait_for(pe, max_read, NMAX * GROUPS, item, n if k == 3 else n - 1)
                w = P * (q + 1)
                for a, i in enumerate(hs):
                    pe.matmul(max_ps[:, bank, a * w:(a + 1) * w], heads[0:96, t, 0, i, q * P:(q + 1) * P],
                              heads[0:96, t, 1, i, 0:w], start=(a == 0), stop=False, skip_group_check=True)

            def masks_for_max(t, k):
                q, hs = MAX_UNITS[k]
                bank, w, n = (MAX_AT + 12 * t + k) % 2, P * (q + 1), len(hs)
                tiles = max_ps[:, bank, 0:n * w].rearrange("p (h n) -> p h n", h=n)[:, :, w - P:w]
                pe.matmul(tiles, identb[:, :], mask_q[:, 0:n, :], start=False, stop=True,
                          skip_group_check=True).then_inc(max_done, 1)

            def emit(window):
                for s in range(SLOTS):
                    for t in range(GROUPS):
                        for item, k in due(window, s, SLOTS, B, MAX_AT + 12 * t, 12):
                            if k in MAX_UNITS:
                                scores_for_max(item, t, k)
                    for n, (kind, t) in enumerate(UNITS):
                        a = acts["x" if kind == "q" else "c"]
                        for item, j in due(window, s, SLOTS, B, LIN + 4 * n, 4):
                            if n in (0, UNITS.index(("q", 0))):
                                wait_for(pe, lo_done, NCHUNK, item, NW + (KT if kind == "q" else 0) + j + 1)
                            if j == 0:
                                wait_for(pe, lin_out, len(UNITS), item, n - 1)
                            for m, (aw, aa) in enumerate(((0, 0), (0, 1), (1, 0))):
                                if kind == "v":
                                    last = pe.matmul(lin_ps[:, n % 2, :], a[:, aw, j, t * P:(t + 1) * P],
                                                     W[kind][:, aa, j, :], start=(j == 0 and m == 0),
                                                     stop=(j == KT - 1 and m == 2))
                                else:
                                    last = pe.matmul(lin_ps[:, n % 2, :], W[kind][:, aw, j, t * P:(t + 1) * P],
                                                     a[:, aa, j, :], start=(j == 0 and m == 0),
                                                     stop=(j == KT - 1 and m == 2))
                            last.then_inc(lin_step, 1)
                    for item, k in due(window, s, SLOTS, B, ST_AT, SLOTS):
                        t, i, c = k // 12, k // 3 % 4, k % 3
                        if k % 12 == 0:
                            wait_for(pe, rows_loaded[t % 2], 64, item, 32 * (t // 2 + 1))
                        wait_for(pe, exp_done, SLOTS, item, k + 1 - 2)
                        for m, (kt, at) in enumerate(ST_UNITS[c]):
                            w = S - kt * P
                            pe.matmul(st_ps[:, k % 2, at:at + w], heads[0:98, t, 1, i, kt * P:(kt + 1) * P],
                                      heads[0:98, t, 0, i, kt * P:S], start=(m == 0), stop=False,
                                      skip_group_check=True)
                    for t in range(GROUPS):
                        for item, k in due(window, s, SLOTS, B, MAX_AT + 12 * t, 12):
                            if k in MAX_UNITS:
                                masks_for_max(t, k)
                    for item, k in due(window, s, SLOTS, B, PV_AT, SLOTS):
                        h, c = k // 3, k % 3
                        if k == 0:
                            wait_for(pe, v_lo, QT, item, QT)
                        if c == 0:
                            wait_for(pe, o_read, HEADS, item, h - 1)
                        wait_for(pe, pl_done, SLOTS, item, k + 1)
                        for m, (kt, at) in enumerate(ST_UNITS[c]):
                            for q in range(kt, QT):
                                col = at + (q - kt) * P
                                o = o_ps[:, h % 2, q * VW:(q + 1) * VW]
                                v = V[:, item.parity, kt, h, :]
                                pe.matmul(o[:, 0:3 * HD + 1], prob_hi[:, k % 4, col:col + P], v[:, 0:3 * HD + 1],
                                          start=(k % 3 == 0 and q == 0), stop=False, skip_group_check=True)
                                last = pe.matmul(o[:, HD:3 * HD + 1], prob_lo[:, k % 4, col:col + P],
                                                 v[:, HD:3 * HD + 1], start=False, stop=(c == 2),
                                                 skip_group_check=True)
                        last.then_inc(pv_done, 1)
                    for item, k in due(window, s, SLOTS, B, ST_AT, SLOTS):
                        for kt, at in ST_UNITS[k % 3]:
                            last = pe.matmul(st_ps[:, k % 2, at:at + P], identb[:, :], mask_k[:, :],
                                             start=False, stop=True, skip_group_check=True)
                        last.then_inc(st_done, 1)
                    for t in range(GROUPS):
                        for item, _ in due(window, s, SLOTS, B, ROW_AT + 12 * t):
                            bank = (ROW_AT + 12 * t) % 2
                            wait_for(pe, parts_ready, GROUPS, item, t + 1)
                            if isinstance(item.n, int) and item.n == B - 1 and t == GROUPS - 1:
                                wait_for(pe, max_read, NMAX * GROUPS, item, NMAX * (t + 1))
                            else:
                                wait_for(pe, max_read, NMAX * GROUPS, item, NMAX * (t + 1) + 1)
                            for q in range(QT):
                                last = pe.transpose(max_ps[0:8, bank, q * P:(q + 1) * P],
                                                    negmax_parts[:, t % 2, q, :, :].rearrange("p a h -> p (a h)"),
                                                    ident[:, :])
                            last.then_inc(rows_done, 1)

            run_windows(pe, B, emit)


def feed(nc, ctx_rows, x, wo, w1, w2, b1, vectors, out):
    N, D = x.shape
    FF = w1.shape[1]
    KT, FT = D // P, FF // P
    U = 2
    T = U * P
    CHUNKS = N // T
    SLOTS = FT
    assert D == 512 and FT == 16 and N % T == 0 and CHUNKS % 2 == 0 and CHUNKS > BACK

    LOAD = 0
    ADD_BO = 2
    OTR = 2
    PROJ = 5
    RES = 7
    NORM1 = 10
    X1TR = 13
    FFN1 = 16
    FFN2 = FFN1 + 2
    RES2 = FFN2 + FT
    STORE = RES2 + 4
    W1Q = FF // 512
    RAW = 4
    PEELED = 4
    FRONT_VECTORS = ("bo", "g1", "be1")
    BACK_VECTORS = ("b2", "g2", "be2")

    with ExitStack() as stack:
        def sb(name, shape, dt):
            return stack.enter_context(nc.sbuf_tensor(name, shape, dt))

        def sem(name):
            return stack.enter_context(nc.semaphore(name))

        Wo = sb("Wo", [P, 2, KT, D], F32R)
        W1 = sb("W1", [P, 2, KT, FF], F32R)
        W2 = sb("W2", [P, 2, FT, D], F32R)
        raw = sb("raw2", [P, RAW, D], F32)
        turned = sb("turned", [P, 2, 2, KT, T], F32R)
        o_in = sb("o_in", [P, U, D], F32)
        x_in = sb("x_in", [P, U, D], F32)
        x1 = sb("x1", [P, 2, U, D], F32)
        hf = sb("hf", [P, 2, T], F32)
        hs = sb("hs", [P, 4, 2, T], F32R)
        y = sb("y", [P, U, D], F32)
        stats = sb("stats", [P, 2, U, 6], F32)
        mv = sb("mv", [P, 2, U, 2], F32)
        gate = sb("gate", [P, 2, 1], F32)
        sd = sb("sd", [P, 2, U], F32)
        ve = sb("ve", [P, 2, U], F32)
        rs = sb("rs", [P, 2, 3, U], F32)
        b1c = sb("b1c", [P, FT], F32)
        vec = {v: sb("vec_" + v, [P, D], F32) for v in vectors}
        ident = sb("ident2", [P, P], F32)

        acc = stack.enter_context(nc.psum_tensor("acc", [P, 2, U, 512], F32))
        h_ps = stack.enter_context(nc.psum_tensor("h_ps", [P, 2, 512], F32))
        front = stack.enter_context(nc.psum_tensor("front", [P, 2, 512], F32))

        made = sem("made")
        front_loaded = sem("front_loaded")
        back_loaded = sem("back_loaded")
        raw_loaded = [sem(f"w_loaded{i}") for i in range(RAW)]
        w_hi = sem("w_hi")
        w_lo = sem("w_lo")
        o_loaded = sem("o_loaded")
        x_loaded = sem("x_loaded")
        bo_added = sem("bo_added")
        turned_ps = sem("turned_ps")
        turned_hi = sem("turned_hi")
        turned_lo = sem("turned_lo")
        proj_done = sem("proj_done")
        res_done = sem("res_done")
        ln_step = [sem("ln1_step"), sem("ln2_step")]
        ln_root = [sem("ln1_root"), sem("ln2_root")]
        ln_var = [sem("ln1_var"), sem("ln2_var")]
        ln_sd = [sem("ln1_sd"), sem("ln2_sd")]
        ln_out = [sem("ln1_out"), sem("ln2_out")]
        aff_step = [sem("aff1_step"), sem("aff2_step")]
        aff_out = [sem("aff1_out"), sem("aff2_out")]
        b2_added = sem("b2_added")
        h_done = sem("h_done")
        h_out = sem("h_out")
        h_lo = sem("h_lo")
        ffn_done = sem("ffn_done")
        y_done = sem("y_done")
        y_stored = sem("y_stored")

        chunks = [(wo.rearrange("(k p) n -> k p n", p=P)[j], Wo[:, :, j, :]) for j in range(KT)]
        for q in range(W1Q):
            chunks += [(w1[j * P:(j + 1) * P, q * 512:(q + 1) * 512], W1[:, :, j, q * 512:(q + 1) * 512])
                       for j in range(KT)]
            chunks += [(w2.rearrange("(k p) n -> k p n", p=P)[f], W2[:, :, f, :])
                       for f in range(q * FT // W1Q, (q + 1) * FT // W1Q)]

        def w1_chunks(f):
            q = f // (FT // W1Q)
            return KT + q * (KT + FT // W1Q) + KT

        def w2_chunks(f):
            return w1_chunks(f) + f % (FT // W1Q) + 1

        def split_slot(n):
            return OTR + 1 if n < KT else PROJ + (n - KT) * 3 // 4

        def weights_due(window, slot):
            if isinstance(window[0], int) and window[0] < BACK:
                return [n for n in range(len(chunks)) if split_slot(n) == slot + SLOTS * window[0]]
            return []

        LNS = 2 * U + 5

        block = stack.enter_context(nc.Block())

        @block.sync
        def _(sp):
            def load_weights(n):
                if n < len(chunks):
                    if n >= RAW:
                        sp.wait_ge(w_lo, n - RAW + 1)
                    sp.dma_start(raw[:, n % RAW, :], chunks[n][0]).then_inc(raw_loaded[n % RAW], 16)

            def load_vectors(names, loaded):
                for v in names:
                    sp.dma_start(vec[v][:, :], vectors[v].rearrange("(a n) -> a n", a=1).to_broadcast([P, D])
                                 ).then_inc(loaded, 16)

            def rows(a, item):
                if isinstance(item.n, int):
                    r = a[item.n * T:(item.n + 1) * T, :]
                else:
                    r = a[bass.ds(sp.snap(item.n * T), T), :]
                return r.rearrange("(u p) n -> p u n", p=P)

            def emit(window):
                for s in range(SLOTS):
                    for item, _ in due(window, s, SLOTS, CHUNKS, LOAD):
                        src_o, src_x = rows(ctx_rows, item), rows(x, item)
                        wait_for_all(sp, (turned_ps, 2 * U, item, -U), (res_done, U, item, 0))
                        sp.dma_start(o_in[:, :, :], src_o).then_inc(o_loaded, 16)
                        sp.dma_start(x_in[:, :, :], src_x).then_inc(x_loaded, 16)
                        if isinstance(item.n, int) and item.n == 0:
                            for n in range(RAW):
                                load_weights(n)
                            load_vectors(FRONT_VECTORS, front_loaded)
                            sp.dma_start(b1c[:, :], b1).then_inc(front_loaded, 16)
                    for n in weights_due(window, s):
                        load_weights(n + RAW)
                        if n == 2 * KT - 1:
                            load_vectors(BACK_VECTORS, back_loaded)
                    for item, _ in due(window, s, SLOTS, CHUNKS, STORE):
                        dst = rows(out, item)
                        wait_for_all(sp, (aff_out[1], U, item, U))
                        sp.dma_start(dst, y[:, :, :]).then_inc(y_stored, 16)

            run_windows(sp, CHUNKS, emit, PEELED)
            sp.wait_ge(y_stored, 16 * CHUNKS)

        @block.gpsimd
        def _(pool):
            pool.memset(ident[:, :], 0.0).then_inc(made, 1)
            pool.wait_ge(made, 1)
            pool.affine_select(out=ident[:, :], in_=ident[:, :], compare_op=ALU.not_equal, fill=1.0,
                               base=0, pattern=[[-1, P]], channel_multiplier=1).then_inc(made, 1)
            pool.wait_ge(front_loaded, 16 * (len(FRONT_VECTORS) + 1))

            def affine(norm, item, u, tile):
                wait_for(pool, ln_out[norm], U, item, u + 1)
                pool.tensor_tensor(tile, tile, vec[f"g{norm + 1}"][:, :], ALU.mult).then_inc(aff_step[norm], 1)
                wait_for(pool, aff_step[norm], U, item, u + 1)
                pool.tensor_tensor(tile, tile, vec[f"be{norm + 1}"][:, :], ALU.add).then_inc(aff_out[norm], 1)

            def emit(window):
                for s in range(SLOTS):
                    for u in range(U):
                        for item, _ in due(window, s, SLOTS, CHUNKS, ADD_BO + u):
                            wait_for(pool, x_loaded, 16, item, 16)
                            pool.tensor_tensor(x_in[:, u, :], x_in[:, u, :], vec["bo"][:, :], ALU.add
                                               ).then_inc(bo_added, 1)
                        for item, _ in due(window, s, SLOTS, CHUNKS, NORM1 + 1 + u):
                            affine(0, item, u, x1[:, item.parity, u, :])
                        for item, _ in due(window, s, SLOTS, CHUNKS, X1TR + 1 + u):
                            wait_for(pool, turned_ps, 2 * U, item, U + u + 1)
                            if isinstance(item.n, int) and item.n == 0:
                                pool.wait_ge(back_loaded, 16 * len(BACK_VECTORS))
                            t = x1[:, item.parity, u, :]
                            pool.tensor_tensor(t, t, vec["b2"][:, :], ALU.add).then_inc(b2_added, 1)
                        for item, _ in due(window, s, SLOTS, CHUNKS, RES2 + 2 + u):
                            affine(1, item, u, y[:, u, :])

            run_windows(pool, CHUNKS, emit, PEELED)

        @block.scalar
        def _(act):
            def root(norm, item):
                wait_for(act, ln_var[norm], 1, item, 1)
                act.activation(sd[:, norm, :], ve[:, norm, :], ACT.Sqrt).then_inc(ln_sd[norm], 1)

            def emit(window):
                for s in range(SLOTS):
                    for kind, at in ((0, OTR), (1, X1TR)):
                        for u in range(U):
                            for item, _ in due(window, s, SLOTS, CHUNKS, at + (1 + 2 * u, u)[kind]):
                                n = U * kind + u
                                wait_for(act, turned_ps, 2 * U, item, n + 1)
                                if kind:
                                    wait_for(act, proj_done, U, item, U)
                                else:
                                    wait_for(act, h_done, FT, item, -FT)
                                act.activation(turned[:, item.parity, 0, :, u * P:(u + 1) * P],
                                               front[:, n % 2, :].rearrange("p (k t) -> p k t", t=P), ACT.Copy
                                               ).then_inc(turned_hi, 1)
                    for n in weights_due(window, s):
                        act.wait_ge(raw_loaded[n % RAW], 16 * (n // RAW + 1))
                        act.activation(chunks[n][1][:, 0, :], raw[:, n % RAW, :], ACT.Copy).then_inc(w_hi, 1)
                    for item, _ in due(window, s, SLOTS, CHUNKS, NORM1):
                        root(0, item)
                    for item, _ in due(window, s, SLOTS, CHUNKS, RES2 + 1):
                        root(1, item)
                    for item, f in due(window, s, SLOTS, CHUNKS, FFN1, FT):
                        if isinstance(item.n, int) and item.n == 0 and f == 0:
                            act.wait_ge(front_loaded, 16 * (len(FRONT_VECTORS) + 1))
                        wait_for(act, h_done, FT, item, f + 1)
                        wait_for(act, h_lo, FT, item, f + 1 - 2)
                        wait_for(act, ffn_done, FT, item, f + 1 - 4)
                        act.activation(hf[:, f % 2, :], h_ps[:, f % 2, 0:T], ACT.Relu,
                                       bias=b1c[:, f:f + 1])
                        act.activation(hs[:, f % 4, 0, :], h_ps[:, f % 2, 0:T], ACT.Relu,
                                       bias=b1c[:, f:f + 1]).then_inc(h_out, 1)

            run_windows(act, CHUNKS, emit, PEELED)

        @block.vector
        def _(dve):
            def statistics(norm, item, u, tile):
                dve.bn_stats(stats[:, norm, u, :], tile).then_inc(ln_step[norm], 1)

            def variance(norm, item):
                wait_for(dve, ln_step[norm], LNS, item, U)
                dve.tensor_copy(gate[:, norm, :], stats[:, norm, 0, 0:1]).then_inc(ln_step[norm], 1)
                for u in range(U):
                    dve.bn_aggr(mv[:, norm, u, :], stats[:, norm, u, :]).then_inc(ln_step[norm], 1)
                wait_for(dve, ln_step[norm], LNS, item, 2 * U + 1)
                dve.tensor_scalar(ve[:, norm, :], mv[:, norm, :, 1], LN_EPS, None, ALU.add).then_inc(ln_var[norm], 1)

            def normalise(norm, item, tiles):
                r, t, z = rs[:, norm, 0, :], rs[:, norm, 1, :], rs[:, norm, 2, :]
                wait_for(dve, ln_sd[norm], 1, item, 1)
                dve.reciprocal(r, sd[:, norm, :]).then_inc(ln_step[norm], 1)
                wait_for(dve, ln_step[norm], LNS, item, 2 * U + 2)
                dve.tensor_tensor(t, r, r, ALU.mult).then_inc(ln_step[norm], 1)
                wait_for(dve, ln_step[norm], LNS, item, 2 * U + 3)
                dve.tensor_tensor(t, t, ve[:, norm, :], ALU.mult).then_inc(ln_step[norm], 1)
                wait_for(dve, ln_step[norm], LNS, item, 2 * U + 4)
                dve.tensor_scalar(t, t, -0.5, 1.5, ALU.mult, ALU.add).then_inc(ln_step[norm], 1)
                wait_for(dve, ln_step[norm], LNS, item, 2 * U + 5)
                dve.tensor_tensor(z, r, t, ALU.mult).then_inc(ln_root[norm], 1)
                wait_for(dve, ln_root[norm], 1, item, 1)
                for u, tile in enumerate(tiles):
                    dve.tensor_scalar(tile, tile, mv[:, norm, u, 0:1], z[:, u:u + 1], ALU.subtract, ALU.mult
                                      ).then_inc(ln_out[norm], 1)

            def emit(window):
                for s in range(SLOTS):
                    for kind, at in ((0, OTR), (1, X1TR)):
                        for u in range(U):
                            for item, _ in due(window, s, SLOTS, CHUNKS, at + (1 + 2 * u, u)[kind]):
                                n = U * kind + u
                                wait_for(dve, turned_hi, 2 * U, item, n + 1)
                                both = turned[:, item.parity, :, :, u * P:(u + 1) * P]
                                dve.tensor_tensor(both[:, 1, :, :], front[:, n % 2, :].rearrange("p (k t) -> p k t", t=P),
                                                  both[:, 0, :, :], ALU.subtract).then_inc(turned_lo, 1)
                    for n in weights_due(window, s):
                        dve.wait_ge(w_hi, n + 1)
                        dst = chunks[n][1]
                        dve.tensor_tensor(dst[:, 1, :], raw[:, n % RAW, :], dst[:, 0, :], ALU.subtract
                                          ).then_inc(w_lo, 1)
                    for u in range(U):
                        for item, _ in due(window, s, SLOTS, CHUNKS, RES + 2 * u):
                            wait_for(dve, proj_done, U, item, u + 1)
                            wait_for(dve, bo_added, U, item, u + 1)
                            wait_for(dve, y_done, U, item, -U)
                            tile = x1[:, item.parity, u, :]
                            dve.tensor_tensor(tile, front[:, u, :], x_in[:, u, :], ALU.add).then_inc(res_done, 1)
                            wait_for(dve, res_done, U, item, u + 1)
                            statistics(0, item, u, tile)
                            if u == U - 1:
                                variance(0, item)
                    for item, _ in due(window, s, SLOTS, CHUNKS, NORM1):
                        normalise(0, item, [x1[:, item.parity, u, :] for u in range(U)])
                    for item, _ in due(window, s, SLOTS, CHUNKS, RES2):
                        for u in range(U):
                            wait_for(dve, ffn_done, FT, item, FT)
                            wait_for(dve, b2_added, U, item, u + 1)
                            wait_for(dve, y_stored, 16, item, 0)
                            dve.tensor_tensor(y[:, u, :], acc[:, item.parity, u, :], x1[:, item.parity, u, :],
                                              ALU.add).then_inc(y_done, 1)
                            wait_for(dve, y_done, U, item, u + 1)
                            statistics(1, item, u, y[:, u, :])
                        variance(1, item)
                    for item, _ in due(window, s, SLOTS, CHUNKS, RES2 + 1):
                        normalise(1, item, [y[:, u, :] for u in range(U)])
                    for item, f in due(window, s, SLOTS, CHUNKS, FFN1, FT):
                        wait_for(dve, h_out, FT, item, f + 1)
                        dve.tensor_tensor(hs[:, f % 4, 1, :], hf[:, f % 2, :], hs[:, f % 4, 0, :], ALU.subtract
                                          ).then_inc(h_lo, 1)

            run_windows(dve, CHUNKS, emit, PEELED)

        @block.tensor
        def _(pe):
            pe.wait_ge(made, 2)

            def emit(window):
                for s in range(SLOTS):
                    for u in range(U):
                        for item, _ in due(window, s, SLOTS, CHUNKS, OTR + 2 * u):
                            wait_for(pe, o_loaded, 16, item, 16)
                            wait_for(pe, turned_lo, 2 * U, item, u - U + 1)
                            for j in range(KT):
                                last = pe.transpose(front[:, u, j * P:(j + 1) * P], o_in[:, u, j * P:(j + 1) * P],
                                                    ident[:, :])
                            last.then_inc(turned_ps, 1)
                        for item, half in due(window, s, SLOTS, CHUNKS, PROJ + 2 * u, 2):
                            if half == 0:
                                wait_for(pe, turned_lo, 2 * U, item, u + 1)
                                if isinstance(item.n, int) and item.n == 0:
                                    pe.wait_ge(w_lo, KT)
                            for j in range(half * KT // 2, (half + 1) * KT // 2):
                                for m, (aa, aw) in enumerate(((0, 0), (0, 1), (1, 0))):
                                    last = pe.matmul(front[:, u, :], turned[:, item.parity, aa, j, u * P:(u + 1) * P],
                                                     Wo[:, aw, j, :], start=(j == 0 and m == 0),
                                                     stop=(j == KT - 1 and m == 2))
                            if half:
                                last.then_inc(proj_done, 1)
                        for item, _ in due(window, s, SLOTS, CHUNKS, X1TR + u):
                            wait_for(pe, aff_out[0], U, item, u + 1)
                            wait_for(pe, res_done, U, item, u + 1)
                            for j in range(KT):
                                last = pe.transpose(front[:, u, j * P:(j + 1) * P],
                                                    x1[:, item.parity, u, j * P:(j + 1) * P], ident[:, :])
                            last.then_inc(turned_ps, 1)
                    for item, f in due(window, s, SLOTS, CHUNKS, FFN1, FT):
                        if f == 0:
                            wait_for(pe, turned_lo, 2 * U, item, 2 * U)
                        if isinstance(item.n, int) and item.n == 0:
                            pe.wait_ge(w_lo, w1_chunks(f))
                        wait_for(pe, h_out, FT, item, f + 1 - 2)
                        for j in range(KT):
                            for m, (aw, aa) in enumerate(((0, 0), (0, 1), (1, 0))):
                                last = pe.matmul(h_ps[:, f % 2, 0:T], W1[:, aw, j, f * P:(f + 1) * P],
                                                 turned[:, item.parity, aa, j, :], start=(j == 0 and m == 0),
                                                 stop=(j == KT - 1 and m == 2))
                        last.then_inc(h_done, 1)
                    for item, f in due(window, s, SLOTS, CHUNKS, FFN2, FT):
                        if f == 0:
                            wait_for(pe, y_done, U, item, -U)
                        if isinstance(item.n, int) and item.n == 0:
                            pe.wait_ge(w_lo, w2_chunks(f))
                        wait_for(pe, h_lo, FT, item, f + 1)
                        for u in range(U):
                            for m, (aa, aw) in enumerate(((0, 0), (0, 1), (1, 0))):
                                last = pe.matmul(acc[:, item.parity, u, :], hs[:, f % 4, aa, u * P:(u + 1) * P],
                                                 W2[:, aw, f, :], start=(f == 0 and m == 0),
                                                 stop=(f == FT - 1 and m == 2))
                        last.then_inc(ffn_done, 1)

            run_windows(pe, CHUNKS, emit, PEELED)


INPUTS = ["xT", "cT", "x", "Wq", "Wk", "Wv", "Wo", "W1", "W2", "bq", "bk", "bv", "b1",
          "bo", "g1", "be1", "b2", "g2", "be2"]


def build(nc, a, out):
    tokens, d = a["x"].shape
    ctx_rows = nc.dram_tensor("ctx_rows", [tokens, d], F32, kind="Internal").ap()
    attention(nc, a["xT"], a["cT"], {w: a["W" + w] for w in "vkq"}, {w: a["b" + w] for w in "kq"}, a["bv"], ctx_rows)
    feed(nc, ctx_rows, a["x"], a["Wo"], a["W1"], a["W2"], a["b1"],
         {v: a[v] for v in ("bo", "g1", "be1", "b2", "g2", "be2")}, out)


def kernel(**inputs):
    import concourse.bacc as bacc
    from concourse.bass_utils import run_bass_kernel_spmd

    def given(name):
        return np.asarray(inputs[name])

    def columns(v):
        return v.reshape(-1, P).T

    x, ctx = given("x"), given("ctx_1024")
    b, s, d = x.shape
    w = {n: given("L0_xattn_" + n) for n in ("Wq", "Wk", "Wv", "Wo", "W1", "W2", "bq", "bk", "bv", "bo", "b1", "b2",
                                             "ln1_g", "ln1_b", "ln2_g", "ln2_b")}
    layout = {"xT": x.transpose(0, 2, 1), "cT": ctx.transpose(0, 2, 1), "x": x.reshape(b * s, d),
              "Wq": w["Wq"], "Wk": w["Wk"], "Wv": w["Wv"], "Wo": w["Wo"], "W1": w["W1"], "W2": w["W2"],
              "bq": columns(w["bq"]), "bk": columns(w["bk"]), "bv": w["bv"], "b1": columns(w["b1"]),
              "bo": w["bo"], "g1": w["ln1_g"], "be1": w["ln1_b"], "b2": w["b2"], "g2": w["ln2_g"], "be2": w["ln2_b"]}
    nc = bacc.Bacc("TRN2", target_bir_lowering=False, num_devices=1, dynamic_dma_scratch_size=2048)
    arrays, args = {}, {}
    for name in INPUTS:
        arrays["in_" + name] = np.ascontiguousarray(layout[name])
        args[name] = nc.dram_tensor("in_" + name, arrays["in_" + name].shape, F32, kind="ExternalInput").ap()
    out = nc.dram_tensor("out", [b * s, d], F32, kind="ExternalOutput").ap()
    build(nc, args, out)
    result = run_bass_kernel_spmd(nc, [arrays], core_ids=[0])
    return result.results[0]["out"].reshape(b, s, d)
```

```python
import numpy as np

import concourse.bass as bass
from concourse import mybir
from contextlib import ExitStack

F32 = mybir.dt.float32
F32R = mybir.dt.float32r
BF16 = mybir.dt.bfloat16
U32 = mybir.dt.uint32
F16 = mybir.dt.float16
ALU = mybir.AluOpType
ACT = mybir.ActivationFunctionType
AX_X = mybir.AxisListType.X

P = 128
HEADS = 16
MASKED = -1e30
LN_EPS = 1e-5
PROB_BITS = 10
BACK = 2


class Item:

    def __init__(self, n, parity):
        self.n, self.parity = n, parity


def due(window, slot, slots, items, first, span=1):
    n, parity = window
    for back in range(BACK + 1):
        k = slot + slots * back - first
        if 0 <= k < span:
            at = n - back if back else n
            if not isinstance(at, int) or 0 <= at < items:
                yield Item(at, (parity - back) % 2), k


def wait_for(eng, sem, per, item, c):
    if isinstance(item.n, int):
        if per * item.n + c > 0:
            eng.wait_ge(sem, per * item.n + c)
    else:
        eng.wait_ge(sem, item.n * per + c if c else item.n * per)


def wait_for_all(eng, *waits):
    values = []
    for sem, per, item, c in waits:
        if isinstance(item.n, int):
            values.append(per * item.n + c)
        else:
            values.append(eng.snap(eng.to_reg(item.n * per + c)))
    for (sem, _, item, _), value in zip(waits, values):
        if not isinstance(item.n, int) or value > 0:
            eng.wait_ge(sem, value)


def run_windows(eng, items, emit, peeled=BACK):
    for w in range(peeled):
        emit((w, w % 2))
    with eng.Fori(0, (items - peeled) // 2) as pair:
        for parity in range(2):
            emit((pair * 2 + (peeled + parity), parity))
    for w in range(items, items + BACK):
        emit((w, w % 2))


def attention(nc, xT, cT, weights, biases, bv, ctx_rows):
    B, D, S = xT.shape
    KT = D // P
    GROUPS = HEADS // 4
    HD = D // HEADS
    QT = S // P
    VW = 3 * HD + 2
    SLOTS = 12 * GROUPS
    SCALE = float(HD) ** -0.5
    PROB_BIAS = PROB_BITS * float(np.log(2.0))
    assert D == S == 512 and HD == 32 and B % 2 == 0 and B > BACK

    CTX_LOAD = 0
    CTX_SPLIT = 24
    X_LOAD = 28
    X_SPLIT = 37
    LIN = 32
    OUT = LIN + 4
    MAX_AT = LIN + 25
    ROW_AT = MAX_AT + 11
    ST_AT = ROW_AT + 6
    PV_AT = ST_AT + 4
    UNITS = [("v", 0), ("v", 1), ("k", 0), ("q", 0), ("v", 2), ("k", 1), ("q", 1), ("v", 3),
             ("k", 2), ("q", 2), ("k", 3), ("q", 3)]
    KQ_INDEX = {u: n for n, u in enumerate(u for u in UNITS if u[0] != "v")}
    GROUP_READY = {t: OUT + 4 * UNITS.index(("q", t)) + 1 for t in range(GROUPS)}
    MAX_UNITS = [(0, (0, 1, 2, 3)), (1, (0, 1)), (1, (2, 3)), (2, (0,)), (2, (1,)), (2, (2,)), (2, (3,)),
                 (3, (0,)), (3, (1,)), (3, (2,)), (3, (3,))]
    NMAX = len(MAX_UNITS)
    ST_UNITS = [((0, 0),), ((1, 0), (3, 3 * P)), ((2, 0),)]
    ST_WIDTH = [4 * P, 4 * P, 2 * P]
    NW = 3 * KT
    NCHUNK = 2 * KT
    RAW = 4
    PROBS = 4

    with ExitStack() as stack:
        def sb(name, shape, dt):
            return stack.enter_context(nc.sbuf_tensor(name, shape, dt))

        def sem(name):
            return stack.enter_context(nc.semaphore(name))

        W = {w: sb(f"w{w}", [P, 2, KT, D], F32R) for w in "vkq"}
        acts = {"c": sb("ctxT", [P, 2, KT, S], F32R), "x": sb("xT", [P, 2, KT, S], F32R)}
        heads = sb("heads", [P, GROUPS, 2, 4, S], F32R)
        raw = sb("raw", [P, RAW, D], F32)
        stage = sb("stage", [P, 2, 2, 2, S], F32R)
        vf = sb("vf", [P, D], F32)
        V = sb("V", [P, 2, QT, HEADS, VW], BF16)
        probs = sb("probs", [P, PROBS, S], F32)
        prob_hi = sb("prob_hi", [P, 4, S], F16)
        prob_lo = sb("prob_lo", [P, 4, S], F16)
        maxima = sb("maxima", [P, 2, QT, 4], F32)
        negmax = sb("negmax", [P, QT, 4], F32)
        negmax_parts = sb("negmax_parts", [P, 2, 4, QT], F32)
        rows = sb("rows", [P, 2, 32], F32)
        osum = sb("osum", [P, QT, HD], F32)
        den = sb("den", [P, QT], F32)
        rden = sb("rden", [P, QT], F32)
        onorm = sb("onorm", [P, 2, QT, 4, HD], F32)
        bias = {"k": sb("bk", [P, GROUPS], F32), "q": sb("bq", [P, GROUPS], F32)}
        bvb = sb("bvb", [P, D], F32)
        identb = sb("identb", [P, P], BF16)
        mask_q = sb("mask_q", [P, 4, P], BF16)
        mask_k = sb("mask_k", [P, 2, P], BF16)

        lin_ps = stack.enter_context(nc.psum_tensor("lin_ps", [P, 2, 512], F32))
        max_ps = stack.enter_context(nc.psum_tensor("max_ps", [P, 2, 512], F32))
        st_ps = stack.enter_context(nc.psum_tensor("st_ps", [P, 2, 512], F32))
        o_ps = stack.enter_context(nc.psum_tensor("o_ps", [P, 2, 512], F32))

        consts = sem("consts")
        const_loaded = sem("const_loaded")
        raw_loaded = [sem(f"raw_loaded{i}") for i in range(RAW)]
        hi_done = sem("hi_done")
        lo_done = sem("lo_done")
        lin_step = sem("lin_step")
        kq_hi = sem("kq_hi")
        lin_out = sem("lin_out")
        v_hi = sem("v_hi")
        v_rest = sem("v_rest")
        v_mid = sem("v_mid")
        v_lo = sem("v_lo")
        heads_loaded = [sem(f"heads_loaded{t}") for t in range(GROUPS)]
        max_done = sem("max_done")
        max_read = sem("max_read")
        neg_step = sem("neg_step")
        rows_ready = sem("rows_ready")
        rows_loaded = [sem(f"rows_loaded{i}") for i in range(2)]
        st_done = sem("st_done")
        exp_done = sem("exp_done")
        pl_done = sem("pl_done")
        pv_done = sem("pv_done")
        o_step = sem("o_step")
        o_read = sem("o_read")
        o_out = sem("o_out")
        stored = [sem(f"stored{i}") for i in range(2)]

        def chunk_of(kind, item, j):
            return NW + j + (KT if kind == "x" else 0)

        block = stack.enter_context(nc.Block())

        @block.sync
        def _(sp):
            def load(dst_n, src, item, c):
                wait_for_all(sp, (lo_done, NCHUNK, item, c - RAW + 1))
                sp.dma_start(raw[:, dst_n, :], src).then_inc(raw_loaded[dst_n], 16)

            start = Item(0, 0)
            for n, w in enumerate("vkq"):
                view = weights[w].rearrange("(k p) n -> k p n", p=P)
                for j in range(KT):
                    c = n * KT + j
                    load(c % RAW, view[j], start, c)
            for w in "kq":
                sp.dma_start(bias[w][:, :], biases[w]).then_inc(const_loaded, 16)
            sp.dma_start(bvb[:, :], bv.rearrange("(a n) -> a n", a=1).to_broadcast([P, D])).then_inc(const_loaded, 16)

            def source(a, item, j):
                if isinstance(item.n, int):
                    return a[item.n, j * P:(j + 1) * P, :]
                return a[bass.ds(sp.snap(item.n), 1), j * P:(j + 1) * P, :].rearrange("a p s -> (a p) s")

            def emit(window):
                for s in range(SLOTS):
                    for j in range(KT):
                        for item, _ in due(window, s, SLOTS, B, CTX_LOAD + 2 * j):
                            load((NW + j) % RAW, source(cT, item, j), item, NW + j)
                        for item, _ in due(window, s, SLOTS, B, X_LOAD + 2 * j):
                            load((NW + KT + j) % RAW, source(xT, item, j), item, NW + KT + j)
                    for t in range(GROUPS):
                        for item, _ in due(window, s, SLOTS, B, GROUP_READY[t]):
                            wait_for_all(sp, (lin_out, len(UNITS), item, UNITS.index(("q", t)) + 1),
                                         (st_done, SLOTS, item, 12 * t + 12 - SLOTS))
                            for part in range(3):
                                for i in range(4):
                                    four = stage[32 * i:32 * i + 32, t % 2, :, :, :].rearrange("p a b n -> p (a b) n")
                                    pick = (four[:, 0:3:2, :], four[:, 1:3, :], four[:, 0:4:3, :])[part]
                                    sp.dma_start(heads[32 * part:32 * part + 32, t, :, i, :].bitcast(F32),
                                                 pick.bitcast(F32)).then_inc(heads_loaded[t], 16)
                    for t in range(GROUPS):
                        for item, _ in due(window, s, SLOTS, B, PV_AT + 12 * t + 14):
                            f = t * P
                            if isinstance(item.n, int):
                                dst = ctx_rows[item.n * S:(item.n + 1) * S, f:f + P]
                            else:
                                dst = ctx_rows[bass.ds(sp.snap(item.n * S), S), f:f + P]
                            wait_for_all(sp, (o_out, HEADS, item, 4 * t + 4))
                            sp.dma_start(dst.rearrange("(q p) n -> p q n", p=P),
                                         onorm[:, t % 2, :, :, :].rearrange("p q h d -> p q (h d)")
                                         ).then_inc(stored[t % 2], 16)
                    for t in range(GROUPS):
                        for item, _ in due(window, s, SLOTS, B, ROW_AT + 12 * t):
                            wait_for_all(sp, (rows_ready, GROUPS, item, t + 1))
                            both = heads[96:98, t, 0, :, :].bitcast(F32).rearrange("p h (q a n) -> p (h q) a n",
                                                                                   a=P // 32, n=32)
                            for a in range(P // 32):
                                sp.dma_start(both[:, :, a, :], rows[32 * a:32 * a + 32, t % 2, :]
                                             ).then_inc(rows_loaded[t % 2], 16)

            run_windows(sp, B, emit)
            for i in range(2):
                sp.wait_ge(stored[i], 16 * B * GROUPS // 2)

        @block.gpsimd
        def _(pool):
            zeros = vf[:, 0:P // 2].bitcast(BF16)
            pool.memset(vf[:, 0:P // 2], 0.0).then_inc(consts, 1)
            pool.wait_ge(consts, 1)
            pool.memset(heads[96:98, :, 1, :, :].bitcast(F32), 1.0).then_inc(consts, 1)
            pool.wait_ge(consts, 2)
            pool.memset(V[:, :, :, :, 3 * HD:VW], 1.0).then_inc(consts, 1)
            pool.wait_ge(consts, 3)
            pool.affine_select(out=identb[:, :], in_=zeros, compare_op=ALU.not_equal, fill=1.0,
                               base=0, pattern=[[-1, P]], channel_multiplier=1).then_inc(consts, 1)
            for i in range(4):
                pool.affine_select(out=mask_q[:, i, :], in_=zeros, compare_op=ALU.is_gt, fill=MASKED,
                                   base=0, pattern=[[-1, P]], channel_multiplier=1).then_inc(consts, 1)
            for i in range(2):
                pool.affine_select(out=mask_k[:, i, :], in_=zeros, compare_op=ALU.is_gt, fill=MASKED,
                                   base=0, pattern=[[1, P]], channel_multiplier=-1).then_inc(consts, 1)

            def emit(window):
                for s in range(SLOTS):
                    for item, k in due(window, s, SLOTS, B, ST_AT, SLOTS):
                        w = ST_WIDTH[k % 3]
                        wait_for(pool, exp_done, SLOTS, item, k + 1)
                        wait_for(pool, pv_done, SLOTS, item, k + 1 - 4)
                        pool.tensor_tensor(prob_lo[:, k % 4, 0:w], probs[:, k % PROBS, 0:w],
                                           prob_hi[:, k % 4, 0:w], ALU.subtract).then_inc(pl_done, 1)

            run_windows(pool, B, emit)

        @block.scalar
        def _(act):
            def split(item, c, dst):
                wait_for(act, raw_loaded[c % RAW], 16 * NCHUNK // RAW, item, 16 * (c // RAW + 1))
                act.activation(dst, raw[:, c % RAW, :], ACT.Copy).then_inc(hi_done, 1)

            start = Item(0, 0)
            for n, w in enumerate("vkq"):
                for j in range(KT):
                    split(start, n * KT + j, W[w][:, 0, j, :])
            act.wait_ge(const_loaded, 48)

            def emit(window):
                for s in range(SLOTS):
                    for n, (kind, t) in enumerate(UNITS):
                        if kind == "v":
                            for item, _ in due(window, s, SLOTS, B, OUT + 4 * n + 1):
                                wait_for(act, lin_out, len(UNITS), item, n + 1)
                                wait_for(act, pv_done, SLOTS, item, -SLOTS)
                                act.activation(V[:, item.parity, t, :, HD:2 * HD],
                                               vf[:, :].rearrange("p (h d) -> p h d", d=HD), ACT.Copy
                                               ).then_inc(v_hi, 1)
                            for item, _ in due(window, s, SLOTS, B, OUT + 4 * n + 3):
                                wait_for(act, v_rest, QT, item, t + 1)
                                act.activation(V[:, item.parity, t, :, 2 * HD:3 * HD],
                                               vf[:, :].rearrange("p (h d) -> p h d", d=HD), ACT.Copy
                                               ).then_inc(v_mid, 1)
                        else:
                            for item, _ in due(window, s, SLOTS, B, OUT + 4 * n):
                                wait_for(act, lin_step, SLOTS, item, 4 * n + 4)
                                wait_for(act, heads_loaded[(t - 2) % GROUPS], 192, item, 192 if t > 1 else 0)
                                act.activation(stage[:, t % 2, "qk".index(kind), 0, :], lin_ps[:, n % 2, :], ACT.Identity,
                                               bias=bias[kind][:, t:t + 1]).then_inc(kq_hi, 1)
                    for j in range(KT):
                        for item, _ in due(window, s, SLOTS, B, CTX_SPLIT + 2 * j):
                            wait_for(act, lin_step, SLOTS, item, 4 * UNITS.index(("k", 3)) + j + 1 - SLOTS)
                            split(item, NW + j, acts["c"][:, 0, j, :])
                        for item, _ in due(window, s, SLOTS, B, X_SPLIT + 2 * j):
                            wait_for(act, lin_step, SLOTS, item, 4 * UNITS.index(("q", 3)) + j + 1 - SLOTS)
                            split(item, NW + KT + j, acts["x"][:, 0, j, :])
                    for item, k in due(window, s, SLOTS, B, ST_AT, SLOTS):
                        w = ST_WIDTH[k % 3]
                        wait_for(act, st_done, SLOTS, item, k + 1)
                        wait_for(act, pl_done, SLOTS, item, k + 1 - PROBS)
                        wait_for(act, pv_done, SLOTS, item, k + 1 - 4)
                        act.activation(probs[:, k % PROBS, 0:w], st_ps[:, k % 2, 0:w], ACT.Exp, bias=PROB_BIAS,
                                       scale=SCALE)
                        act.activation(prob_hi[:, k % 4, 0:w], st_ps[:, k % 2, 0:w], ACT.Exp, bias=PROB_BIAS,
                                       scale=SCALE
                                       ).then_inc(exp_done, 1)

            run_windows(act, B, emit)

        @block.vector
        def _(dve):
            def split(item, c, hi, lo):
                wait_for(dve, hi_done, NCHUNK, item, c + 1)
                dve.tensor_tensor(lo, raw[:, c % RAW, :], hi, ALU.subtract).then_inc(lo_done, 1)

            start = Item(0, 0)
            for n, w in enumerate("vkq"):
                for j in range(KT):
                    split(start, n * KT + j, W[w][:, 0, j, :], W[w][:, 1, j, :])
            dve.wait_ge(const_loaded, 48)

            def emit(window):
                for s in range(SLOTS):
                    for n, (kind, t) in enumerate(UNITS):
                        if kind == "v":
                            for item, _ in due(window, s, SLOTS, B, OUT + 4 * n):
                                wait_for(dve, lin_step, SLOTS, item, 4 * n + 4)
                                wait_for(dve, v_lo, QT, item, t)
                                dve.tensor_tensor(vf[:, :], lin_ps[:, n % 2, :], bvb[:, :], ALU.add
                                                  ).then_inc(lin_out, 1)
                            vr = vf[:, :].rearrange("p (h d) -> p h d", d=HD)
                            for item, _ in due(window, s, SLOTS, B, OUT + 4 * n + 2):
                                wait_for(dve, v_hi, QT, item, t + 1)
                                dve.tensor_tensor(vr, vr, V[:, item.parity, t, :, HD:2 * HD], ALU.subtract
                                                  ).then_inc(v_rest, 1)
                            for item, _ in due(window, s, SLOTS, B, OUT + 4 * n + 4):
                                wait_for(dve, v_mid, QT, item, t + 1)
                                dve.tensor_tensor(V[:, item.parity, t, :, 0:HD], vr,
                                                  V[:, item.parity, t, :, 2 * HD:3 * HD], ALU.subtract
                                                  ).then_inc(v_lo, 1)
                        else:
                            qk = "qk".index(kind)
                            for item, _ in due(window, s, SLOTS, B, OUT + 4 * n + 1):
                                wait_for(dve, kq_hi, len(KQ_INDEX), item, KQ_INDEX[kind, t] + 1)
                                dve.scalar_tensor_tensor(out=stage[:, t % 2, qk, 1, :], in0=lin_ps[:, n % 2, :],
                                                         scalar=bias[kind][:, t:t + 1], in1=stage[:, t % 2, qk, 0, :],
                                                         op0=ALU.add, op1=ALU.subtract).then_inc(lin_out, 1)
                    for h in range(HEADS):
                        t, i = h // 4, h % 4
                        o = o_ps[:, h % 2, 0:QT * VW].rearrange("p (q w) -> p q w", w=VW)
                        for item, _ in due(window, s, SLOTS, B, PV_AT + 3 * h + 3):
                            wait_for(dve, pv_done, SLOTS, item, 3 * h + 3)
                            wait_for(dve, o_out, HEADS, item, h)
                            dve.tensor_scalar(den[:, :], o[:, :, 3 * HD], 1e-30, None, ALU.max).then_inc(o_step, 1)
                            dve.tensor_reduce(osum[:, :, :],
                                              o[:, :, 0:3 * HD].rearrange("p q (c d) -> p q d c", c=3),
                                              AX_X, ALU.add).then_inc(o_read, 1)
                            wait_for(dve, o_step, 2 * HEADS, item, 2 * h + 1)
                            dve.reciprocal(rden[:, :], den[:, :]).then_inc(o_step, 1)
                        for item, _ in due(window, s, SLOTS, B, PV_AT + 3 * h + 4):
                            wait_for(dve, o_read, HEADS, item, h + 1)
                            wait_for(dve, o_step, 2 * HEADS, item, 2 * h + 2)
                            if i == 0:
                                wait_for(dve, stored[t % 2], 32, item, 16 * (t // 2))
                            dve.tensor_tensor(onorm[:, t % 2, :, i, :], osum[:, :, :],
                                              rden[:, :].unsqueeze(2).to_broadcast([P, QT, HD]), ALU.mult
                                              ).then_inc(o_out, 1)
                    for j in range(KT):
                        for item, _ in due(window, s, SLOTS, B, CTX_SPLIT + 2 * j + 1):
                            split(item, NW + j, acts["c"][:, 0, j, :], acts["c"][:, 1, j, :])
                        for item, _ in due(window, s, SLOTS, B, X_SPLIT + 2 * j + 1):
                            split(item, NW + KT + j, acts["x"][:, 0, j, :], acts["x"][:, 1, j, :])
                    for t in range(GROUPS):
                        for item, _ in due(window, s, SLOTS, B, ROW_AT + 12 * t):
                            wait_for(dve, max_read, NMAX * GROUPS, item, NMAX * (t + 1))
                            wait_for(dve, rows_ready, GROUPS, item, t)
                            dve.tensor_scalar(negmax[:, :, :], maxima[:, t % 2, :, :], -1e28, -1.0, ALU.max, ALU.mult
                                              ).then_inc(neg_step, 1)
                            wait_for(dve, neg_step, 3 * GROUPS, item, 3 * t + 1)
                            by_head = negmax[:, :, :].rearrange("p q h -> p h q")
                            hi, lo = negmax_parts[:, 0, :, :], negmax_parts[:, 1, :, :]
                            dve.tensor_copy(hi.bitcast(F32R), by_head).then_inc(neg_step, 1)
                            wait_for(dve, neg_step, 3 * GROUPS, item, 3 * t + 2)
                            dve.tensor_tensor(lo.bitcast(F32R), by_head, hi, ALU.subtract).then_inc(neg_step, 1)
                            wait_for(dve, neg_step, 3 * GROUPS, item, 3 * t + 3)
                            wait_for(dve, rows_loaded[t % 2], 128, item, 64 * (t // 2))
                            dve.transpose(rows[:, t % 2, :].bitcast(U32),
                                          negmax_parts[:, :, :, :].rearrange("p c h q -> p (c h q)").bitcast(U32)
                                          ).then_inc(rows_ready, 1)
                    for t in range(GROUPS):
                        for item, k in due(window, s, SLOTS, B, MAX_AT + 12 * t, 12):
                            if k < NMAX:
                                q, hs = MAX_UNITS[k]
                                n = NMAX * t + k
                                wait_for(dve, max_done, NMAX * GROUPS, item, n + 1)
                                if k == 0:
                                    wait_for(dve, rows_ready, GROUPS, item, t - 1)
                                bank = max_ps[:, (MAX_AT + 12 * t + k) % 2, 0:len(hs) * P * (q + 1)]
                                dve.tensor_reduce(maxima[:, t % 2, q, hs[0]:hs[0] + len(hs)],
                                                  bank.rearrange("p (h n) -> p h n", h=len(hs)), AX_X, ALU.max
                                                  ).then_inc(max_read, 1)

            run_windows(dve, B, emit)

        @block.tensor
        def _(pe):
            pe.wait_ge(consts, 10)

            def scores_for_max(item, t, k):
                q, hs = MAX_UNITS[k]
                bank = (MAX_AT + 12 * t + k) % 2
                n = NMAX * t + k
                if k == 0:
                    wait_for(pe, heads_loaded[t], 192, item, 192)
                wait_for(pe, max_read, NMAX * GROUPS, item, (n, n - 2)[k] if k < 2 else n - 1)
                w = P * (q + 1)
                for a, i in enumerate(hs):
                    pe.matmul(max_ps[:, bank, a * w:(a + 1) * w], heads[0:96, t, 0, i, q * P:(q + 1) * P],
                              heads[0:96, t, 1, i, 0:w], start=(a == 0), stop=False, skip_group_check=True)

            def masks_for_max(t, k):
                q, hs = MAX_UNITS[k]
                bank, w, n = (MAX_AT + 12 * t + k) % 2, P * (q + 1), len(hs)
                tiles = max_ps[:, bank, 0:n * w].rearrange("p (h n) -> p h n", h=n)[:, :, w - P:w]
                pe.matmul(tiles, identb[:, :], mask_q[:, 0:n, :], start=False, stop=True,
                          skip_group_check=True).then_inc(max_done, 1)

            def emit(window):
                for s in range(SLOTS):
                    for n, (kind, t) in enumerate(UNITS):
                        a = acts["x" if kind == "q" else "c"]
                        for item, j in due(window, s, SLOTS, B, LIN + 4 * n, 4):
                            if n in (0, UNITS.index(("q", 0))):
                                wait_for(pe, lo_done, NCHUNK, item, NW + (KT if kind == "q" else 0) + j + 1)
                            if j == 0:
                                wait_for(pe, lin_out, len(UNITS), item, n - 1)
                            for m, (aw, aa) in enumerate(((0, 0), (0, 1), (1, 0))):
                                if kind == "v":
                                    last = pe.matmul(lin_ps[:, n % 2, :], a[:, aw, j, t * P:(t + 1) * P],
                                                     W[kind][:, aa, j, :], start=(j == 0 and m == 0),
                                                     stop=(j == KT - 1 and m == 2))
                                else:
                                    last = pe.matmul(lin_ps[:, n % 2, :], W[kind][:, aw, j, t * P:(t + 1) * P],
                                                     a[:, aa, j, :], start=(j == 0 and m == 0),
                                                     stop=(j == KT - 1 and m == 2))
                            last.then_inc(lin_step, 1)
                    for t in range(GROUPS):
                        for item, k in due(window, s, SLOTS, B, MAX_AT + 12 * t, 12):
                            if k < NMAX:
                                scores_for_max(item, t, k)
                    for item, k in due(window, s, SLOTS, B, ST_AT, SLOTS):
                        t, i, c = k // 12, k // 3 % 4, k % 3
                        if k % 12 == 0:
                            wait_for(pe, rows_loaded[t % 2], 128, item, 64 * (t // 2 + 1))
                        wait_for(pe, exp_done, SLOTS, item, k + 1 - 2)
                        for m, (kt, at) in enumerate(ST_UNITS[c]):
                            w = S - kt * P
                            pe.matmul(st_ps[:, k % 2, at:at + w], heads[0:98, t, 1, i, kt * P:(kt + 1) * P],
                                      heads[0:98, t, 0, i, kt * P:S], start=(m == 0), stop=False,
                                      skip_group_check=True)
                    for t in range(GROUPS):
                        for item, k in due(window, s, SLOTS, B, MAX_AT + 12 * t, 12):
                            if k < NMAX:
                                masks_for_max(t, k)
                    for item, k in due(window, s, SLOTS, B, PV_AT, SLOTS):
                        h, c = k // 3, k % 3
                        if k == 0:
                            wait_for(pe, v_lo, QT, item, QT)
                        if c == 0:
                            wait_for(pe, o_read, HEADS, item, h - 1)
                        wait_for(pe, pl_done, SLOTS, item, k + 1)
                        for m, (kt, at) in enumerate(ST_UNITS[c]):
                            for q in range(kt, QT):
                                col = at + (q - kt) * P
                                o = o_ps[:, h % 2, q * VW:(q + 1) * VW]
                                v = V[:, item.parity, kt, h, :]
                                pe.matmul(o[:, 0:3 * HD + 1], prob_hi[:, k % 4, col:col + P], v[:, 0:3 * HD + 1],
                                          start=(k % 3 == 0 and q == 0), stop=False, skip_group_check=True)
                                last = pe.matmul(o[:, HD:3 * HD + 1], prob_lo[:, k % 4, col:col + P],
                                                 v[:, HD:3 * HD + 1], start=False, stop=(c == 2),
                                                 skip_group_check=True)
                        last.then_inc(pv_done, 1)
                    for item, k in due(window, s, SLOTS, B, ST_AT, SLOTS):
                        unit = ST_UNITS[k % 3]
                        step = unit[-1][1] or S
                        tiles = st_ps[:, k % 2, :].rearrange("p (c n) -> p c n", c=len(unit))[:, :, 0:P] if step == S \
                            else st_ps[:, k % 2, :].rearrange("p (c n) -> p c n", n=P)[:, 0:KT:step // P, :]
                        pe.matmul(tiles, identb[:, :], mask_k[:, 0:len(unit), :],
                                  start=False, stop=True, skip_group_check=True).then_inc(st_done, 1)

            run_windows(pe, B, emit)


def feed(nc, ctx_rows, x, wo, w1, w2, b1, vectors, out):
    N, D = x.shape
    FF = w1.shape[1]
    KT, FT = D // P, FF // P
    U = 2
    T = U * P
    CHUNKS = N // T
    SLOTS = FT
    assert D == 512 and FT == 16 and N % T == 0 and CHUNKS % 2 == 0 and CHUNKS > BACK

    LOAD = 0
    ADD_BO = 2
    OTR = 2
    PROJ = 5
    RES = 7
    NORM1 = 10
    X1TR = 13
    FFN1 = 16
    FFN2 = FFN1 + 2
    RES2 = FFN2 + FT
    STORE = RES2 + 4
    W1Q = FF // 512
    RAW = 4
    PEELED = 4
    FRONT_VECTORS = ("bo", "g1", "be1")
    BACK_VECTORS = ("b2", "g2", "be2")

    with ExitStack() as stack:
        def sb(name, shape, dt):
            return stack.enter_context(nc.sbuf_tensor(name, shape, dt))

        def sem(name):
            return stack.enter_context(nc.semaphore(name))

        Wo = sb("Wo", [P, 2, KT, D], F32R)
        W1 = sb("W1", [P, 2, KT, FF], F32R)
        W2 = sb("W2", [P, 2, FT, D], F32R)
        raw = sb("raw2", [P, RAW, D], F32)
        turned = sb("turned", [P, 2, 2, KT, T], F32R)
        o_in = sb("o_in", [P, U, D], F32)
        o_turned = sb("o_turned", [P, KT, P], F32)
        x_in = sb("x_in", [P, U, D], F32)
        x1 = sb("x1", [P, 2, U, D], F32)
        hf = sb("hf", [P, 2, T], F32)
        hs = sb("hs", [P, 4, 2, T], F32R)
        y = sb("y", [P, U, D], F32)
        stats = sb("stats", [P, 2, U, 6], F32)
        mv = sb("mv", [P, 2, U, 2], F32)
        gate = sb("gate", [P, 2, 1], F32)
        sd = sb("sd", [P, 2, U], F32)
        ve = sb("ve", [P, 2, U], F32)
        rs = sb("rs", [P, 2, 3, U], F32)
        b1c = sb("b1c", [P, FT], F32)
        vec = {v: sb("vec_" + v, [P, D], F32) for v in vectors}
        ident = sb("ident2", [P, P], F32)

        acc = stack.enter_context(nc.psum_tensor("acc", [P, 2, U, 512], F32))
        h_ps = stack.enter_context(nc.psum_tensor("h_ps", [P, 2, 512], F32))
        front = stack.enter_context(nc.psum_tensor("front", [P, 2, 512], F32))

        made = sem("made")
        front_loaded = sem("front_loaded")
        back_loaded = sem("back_loaded")
        raw_loaded = [sem(f"w_loaded{i}") for i in range(RAW)]
        w_hi = sem("w_hi")
        w_lo = sem("w_lo")
        o_loaded = [sem(f"o_loaded{u}") for u in range(U)]
        x_loaded = sem("x_loaded")
        bo_added = sem("bo_added")
        ctx_turned = sem("ctx_turned")
        x1_turned = sem("x1_turned")
        turned_hi = sem("turned_hi")
        turned_lo = sem("turned_lo")
        proj_done = sem("proj_done")
        res_done = sem("res_done")
        ln_step = [sem("ln1_step"), sem("ln2_step")]
        ln_root = [sem("ln1_root"), sem("ln2_root")]
        ln_var = [sem("ln1_var"), sem("ln2_var")]
        ln_sd = [sem("ln1_sd"), sem("ln2_sd")]
        ln_out = [sem("ln1_out"), sem("ln2_out")]
        aff_step = [sem("aff1_step"), sem("aff2_step")]
        aff_out = [sem("aff1_out"), sem("aff2_out")]
        b2_added = sem("b2_added")
        h_done = sem("h_done")
        h_out = sem("h_out")
        h_lo = sem("h_lo")
        ffn_done = sem("ffn_done")
        y_done = sem("y_done")
        y_stored = sem("y_stored")

        chunks = [(wo.rearrange("(k p) n -> k p n", p=P)[j], Wo[:, :, j, :]) for j in range(KT)]
        for q in range(W1Q):
            chunks += [(w1[j * P:(j + 1) * P, q * 512:(q + 1) * 512], W1[:, :, j, q * 512:(q + 1) * 512])
                       for j in range(KT)]
            chunks += [(w2.rearrange("(k p) n -> k p n", p=P)[f], W2[:, :, f, :])
                       for f in range(q * FT // W1Q, (q + 1) * FT // W1Q)]

        def w1_chunks(f):
            q = f // (FT // W1Q)
            return KT + q * (KT + FT // W1Q) + KT

        def w2_chunks(f):
            return w1_chunks(f) + f % (FT // W1Q) + 1

        def split_slot(n):
            return OTR + 1 if n < KT else PROJ + (n - KT) * 3 // 4

        def weights_due(window, slot):
            if isinstance(window[0], int) and window[0] < BACK:
                return [n for n in range(len(chunks)) if split_slot(n) == slot + SLOTS * window[0]]
            return []

        LNS = 2 * U + 5

        block = stack.enter_context(nc.Block())

        @block.sync
        def _(sp):
            def load_weights(n):
                if n < len(chunks):
                    if n >= RAW:
                        sp.wait_ge(w_lo, n - RAW + 1)
                    sp.dma_start(raw[:, n % RAW, :], chunks[n][0]).then_inc(raw_loaded[n % RAW], 16)

            def load_vectors(names, loaded):
                for v in names:
                    sp.dma_start(vec[v][:, :], vectors[v].rearrange("(a n) -> a n", a=1).to_broadcast([P, D])
                                 ).then_inc(loaded, 16)

            def token_rows(a, item):
                if isinstance(item.n, int):
                    return a[item.n * T:(item.n + 1) * T, :]
                return a[bass.ds(sp.snap(item.n * T), T), :]

            def rows(a, item):
                return token_rows(a, item).rearrange("(u p) n -> p u n", p=P)

            def emit(window):
                for s in range(SLOTS):
                    for item, _ in due(window, s, SLOTS, CHUNKS, LOAD):
                        src_o, src_x = token_rows(ctx_rows, item), rows(x, item)
                        wait_for_all(sp, (ctx_turned, U, item, 0), (res_done, U, item, 0))
                        for u in range(U):
                            for b in range(P // 32):
                                src = src_o[u * P:(u + 1) * P, :].rearrange("(a t) (j b f) -> b t j a f",
                                                                            t=32, f=32, b=P // 32)[b]
                                dst = o_in[32 * b:32 * b + 32, u, :].rearrange("t (j a f) -> t j a f", f=32, a=P // 32)
                                sp.dma_start(dst, src).then_inc(o_loaded[u], 16)
                        sp.dma_start(x_in[:, :, :], src_x).then_inc(x_loaded, 16)
                        if isinstance(item.n, int) and item.n == 0:
                            for n in range(RAW):
                                load_weights(n)
                            load_vectors(FRONT_VECTORS, front_loaded)
                            sp.dma_start(b1c[:, :], b1).then_inc(front_loaded, 16)
                    for n in weights_due(window, s):
                        load_weights(n + RAW)
                        if n == 2 * KT - 1:
                            load_vectors(BACK_VECTORS, back_loaded)
                    for item, _ in due(window, s, SLOTS, CHUNKS, STORE):
                        dst = rows(out, item)
                        wait_for_all(sp, (aff_out[1], U, item, U))
                        sp.dma_start(dst, y[:, :, :]).then_inc(y_stored, 16)

            run_windows(sp, CHUNKS, emit, PEELED)
            sp.wait_ge(y_stored, 16 * CHUNKS)

        @block.gpsimd
        def _(pool):
            pool.memset(ident[:, :], 0.0).then_inc(made, 1)
            pool.wait_ge(made, 1)
            pool.affine_select(out=ident[:, :], in_=ident[:, :], compare_op=ALU.not_equal, fill=1.0,
                               base=0, pattern=[[-1, P]], channel_multiplier=1).then_inc(made, 1)
            pool.wait_ge(front_loaded, 16 * (len(FRONT_VECTORS) + 1))

            def affine(norm, item, u, tile):
                wait_for(pool, ln_out[norm], U, item, u + 1)
                pool.tensor_tensor(tile, tile, vec[f"g{norm + 1}"][:, :], ALU.mult).then_inc(aff_step[norm], 1)
                wait_for(pool, aff_step[norm], U, item, u + 1)
                pool.tensor_tensor(tile, tile, vec[f"be{norm + 1}"][:, :], ALU.add).then_inc(aff_out[norm], 1)

            def emit(window):
                for s in range(SLOTS):
                    for u in range(U):
                        for item, _ in due(window, s, SLOTS, CHUNKS, ADD_BO + u):
                            wait_for(pool, x_loaded, 16, item, 16)
                            pool.tensor_tensor(x_in[:, u, :], x_in[:, u, :], vec["bo"][:, :], ALU.add
                                               ).then_inc(bo_added, 1)
                        for item, _ in due(window, s, SLOTS, CHUNKS, NORM1 + 1 + u):
                            affine(0, item, u, x1[:, item.parity, u, :])
                        for item, _ in due(window, s, SLOTS, CHUNKS, X1TR + 1 + u):
                            wait_for(pool, x1_turned, U, item, u + 1)
                            if isinstance(item.n, int) and item.n == 0:
                                pool.wait_ge(back_loaded, 16 * len(BACK_VECTORS))
                            t = x1[:, item.parity, u, :]
                            pool.tensor_tensor(t, t, vec["b2"][:, :], ALU.add).then_inc(b2_added, 1)
                        for item, _ in due(window, s, SLOTS, CHUNKS, RES2 + 2 + u):
                            affine(1, item, u, y[:, u, :])

            run_windows(pool, CHUNKS, emit, PEELED)

        @block.scalar
        def _(act):
            def root(norm, item):
                wait_for(act, ln_var[norm], 1, item, 1)
                act.activation(sd[:, norm, :], ve[:, norm, :], ACT.Sqrt).then_inc(ln_sd[norm], 1)

            def emit(window):
                for s in range(SLOTS):
                    for kind, at in ((0, OTR), (1, X1TR)):
                        for u in range(U):
                            for item, _ in due(window, s, SLOTS, CHUNKS, at + (1 + 2 * u, u)[kind]):
                                n = U * kind + u
                                both = turned[:, item.parity, :, :, u * P:(u + 1) * P]
                                if kind:
                                    wait_for(act, x1_turned, U, item, u + 1)
                                    wait_for(act, proj_done, U, item, U)
                                    whole = front[:, u, :].rearrange("p (k t) -> p k t", t=P)
                                else:
                                    wait_for(act, ctx_turned, U, item, u + 1)
                                    wait_for(act, h_done, FT, item, -FT)
                                    whole = o_turned[:, :, :]
                                act.activation(both[:, 0, :, :], whole, ACT.Copy).then_inc(turned_hi, 1)
                    for n in weights_due(window, s):
                        act.wait_ge(raw_loaded[n % RAW], 16 * (n // RAW + 1))
                        act.activation(chunks[n][1][:, 0, :], raw[:, n % RAW, :], ACT.Copy).then_inc(w_hi, 1)
                    for item, _ in due(window, s, SLOTS, CHUNKS, NORM1):
                        root(0, item)
                    for item, _ in due(window, s, SLOTS, CHUNKS, RES2 + 1):
                        root(1, item)
                    for item, f in due(window, s, SLOTS, CHUNKS, FFN1, FT):
                        if isinstance(item.n, int) and item.n == 0 and f == 0:
                            act.wait_ge(front_loaded, 16 * (len(FRONT_VECTORS) + 1))
                        wait_for(act, h_done, FT, item, f + 1)
                        wait_for(act, h_lo, FT, item, f + 1 - 2)
                        wait_for(act, ffn_done, FT, item, f + 1 - 4)
                        act.activation(hf[:, f % 2, :], h_ps[:, f % 2, 0:T], ACT.Relu,
                                       bias=b1c[:, f:f + 1])
                        act.activation(hs[:, f % 4, 0, :], h_ps[:, f % 2, 0:T], ACT.Relu,
                                       bias=b1c[:, f:f + 1]).then_inc(h_out, 1)

            run_windows(act, CHUNKS, emit, PEELED)

        @block.vector
        def _(dve):
            def statistics(norm, item, u, tile):
                dve.bn_stats(stats[:, norm, u, :], tile).then_inc(ln_step[norm], 1)

            def variance(norm, item):
                wait_for(dve, ln_step[norm], LNS, item, U)
                dve.tensor_copy(gate[:, norm, :], stats[:, norm, 0, 0:1]).then_inc(ln_step[norm], 1)
                for u in range(U):
                    dve.bn_aggr(mv[:, norm, u, :], stats[:, norm, u, :]).then_inc(ln_step[norm], 1)
                wait_for(dve, ln_step[norm], LNS, item, 2 * U + 1)
                dve.tensor_scalar(ve[:, norm, :], mv[:, norm, :, 1], LN_EPS, None, ALU.add).then_inc(ln_var[norm], 1)

            def normalise(norm, item, tiles):
                r, t, z = rs[:, norm, 0, :], rs[:, norm, 1, :], rs[:, norm, 2, :]
                wait_for(dve, ln_sd[norm], 1, item, 1)
                dve.reciprocal(r, sd[:, norm, :]).then_inc(ln_step[norm], 1)
                wait_for(dve, ln_step[norm], LNS, item, 2 * U + 2)
                dve.tensor_tensor(t, r, r, ALU.mult).then_inc(ln_step[norm], 1)
                wait_for(dve, ln_step[norm], LNS, item, 2 * U + 3)
                dve.tensor_tensor(t, t, ve[:, norm, :], ALU.mult).then_inc(ln_step[norm], 1)
                wait_for(dve, ln_step[norm], LNS, item, 2 * U + 4)
                dve.tensor_scalar(t, t, -0.5, 1.5, ALU.mult, ALU.add).then_inc(ln_step[norm], 1)
                wait_for(dve, ln_step[norm], LNS, item, 2 * U + 5)
                dve.tensor_tensor(z, r, t, ALU.mult).then_inc(ln_root[norm], 1)
                wait_for(dve, ln_root[norm], 1, item, 1)
                for u, tile in enumerate(tiles):
                    dve.tensor_scalar(tile, tile, mv[:, norm, u, 0:1], z[:, u:u + 1], ALU.subtract, ALU.mult
                                      ).then_inc(ln_out[norm], 1)

            def emit(window):
                for s in range(SLOTS):
                    for u in range(U):
                        for item, _ in due(window, s, SLOTS, CHUNKS, OTR + 2 * u):
                            wait_for(dve, o_loaded[u], 64, item, 64)
                            wait_for(dve, turned_lo, 2 * U, item, u - (U if u == 0 else 0))
                            dve.transpose(o_turned[:, :, :].bitcast(U32),
                                          o_in[:, u, :].bitcast(U32).rearrange("p (k t) -> p k t", t=P)
                                          ).then_inc(ctx_turned, 1)
                    for kind, at in ((0, OTR), (1, X1TR)):
                        for u in range(U):
                            for item, _ in due(window, s, SLOTS, CHUNKS, at + (1 + 2 * u, u)[kind]):
                                n = U * kind + u
                                wait_for(dve, turned_hi, 2 * U, item, n + 1)
                                both = turned[:, item.parity, :, :, u * P:(u + 1) * P]
                                whole = (o_turned[:, :, :],
                                         front[:, u, :].rearrange("p (k t) -> p k t", t=P))[kind]
                                dve.tensor_tensor(both[:, 1, :, :], whole, both[:, 0, :, :], ALU.subtract
                                                  ).then_inc(turned_lo, 1)
                    for n in weights_due(window, s):
                        dve.wait_ge(w_hi, n + 1)
                        dst = chunks[n][1]
                        dve.tensor_tensor(dst[:, 1, :], raw[:, n % RAW, :], dst[:, 0, :], ALU.subtract
                                          ).then_inc(w_lo, 1)
                    for u in range(U):
                        for item, _ in due(window, s, SLOTS, CHUNKS, RES + 2 * u):
                            wait_for(dve, proj_done, U, item, u + 1)
                            wait_for(dve, bo_added, U, item, u + 1)
                            wait_for(dve, y_done, U, item, -U)
                            tile = x1[:, item.parity, u, :]
                            dve.tensor_tensor(tile, front[:, u, :], x_in[:, u, :], ALU.add).then_inc(res_done, 1)
                            wait_for(dve, res_done, U, item, u + 1)
                            statistics(0, item, u, tile)
                            if u == U - 1:
                                variance(0, item)
                    for item, _ in due(window, s, SLOTS, CHUNKS, NORM1):
                        normalise(0, item, [x1[:, item.parity, u, :] for u in range(U)])
                    for item, _ in due(window, s, SLOTS, CHUNKS, RES2):
                        for u in range(U):
                            wait_for(dve, ffn_done, FT, item, FT)
                            wait_for(dve, b2_added, U, item, u + 1)
                            wait_for(dve, y_stored, 16, item, 0)
                            dve.tensor_tensor(y[:, u, :], acc[:, item.parity, u, :], x1[:, item.parity, u, :],
                                              ALU.add).then_inc(y_done, 1)
                            wait_for(dve, y_done, U, item, u + 1)
                            statistics(1, item, u, y[:, u, :])
                        variance(1, item)
                    for item, _ in due(window, s, SLOTS, CHUNKS, RES2 + 1):
                        normalise(1, item, [y[:, u, :] for u in range(U)])
                    for item, f in due(window, s, SLOTS, CHUNKS, FFN1, FT):
                        wait_for(dve, h_out, FT, item, f + 1)
                        dve.tensor_tensor(hs[:, f % 4, 1, :], hf[:, f % 2, :], hs[:, f % 4, 0, :], ALU.subtract
                                          ).then_inc(h_lo, 1)

            run_windows(dve, CHUNKS, emit, PEELED)

        @block.tensor
        def _(pe):
            pe.wait_ge(made, 2)

            def emit(window):
                for s in range(SLOTS):
                    for u in range(U):
                        for item, half in due(window, s, SLOTS, CHUNKS, PROJ + 2 * u, 2):
                            if half == 0:
                                wait_for(pe, turned_lo, 2 * U, item, u + 1)
                                if isinstance(item.n, int) and item.n == 0:
                                    pe.wait_ge(w_lo, KT)
                            for j in range(half * KT // 2, (half + 1) * KT // 2):
                                for m, (aa, aw) in enumerate(((0, 0), (0, 1), (1, 0))):
                                    last = pe.matmul(front[:, u, :], turned[:, item.parity, aa, j, u * P:(u + 1) * P],
                                                     Wo[:, aw, j, :], start=(j == 0 and m == 0),
                                                     stop=(j == KT - 1 and m == 2))
                            if half:
                                last.then_inc(proj_done, 1)
                        for item, _ in due(window, s, SLOTS, CHUNKS, X1TR + u):
                            wait_for(pe, aff_out[0], U, item, u + 1)
                            wait_for(pe, res_done, U, item, u + 1)
                            for j in range(KT):
                                last = pe.transpose(front[:, u, j * P:(j + 1) * P],
                                                    x1[:, item.parity, u, j * P:(j + 1) * P], ident[:, :])
                            last.then_inc(x1_turned, 1)
                    for item, f in due(window, s, SLOTS, CHUNKS, FFN1, FT):
                        if f == 0:
                            wait_for(pe, turned_lo, 2 * U, item, 2 * U)
                        if isinstance(item.n, int) and item.n == 0:
                            pe.wait_ge(w_lo, w1_chunks(f))
                        wait_for(pe, h_out, FT, item, f + 1 - 2)
                        for j in range(KT):
                            for m, (aw, aa) in enumerate(((0, 0), (0, 1), (1, 0))):
                                last = pe.matmul(h_ps[:, f % 2, 0:T], W1[:, aw, j, f * P:(f + 1) * P],
                                                 turned[:, item.parity, aa, j, :], start=(j == 0 and m == 0),
                                                 stop=(j == KT - 1 and m == 2))
                        last.then_inc(h_done, 1)
                    for item, f in due(window, s, SLOTS, CHUNKS, FFN2, FT):
                        if f == 0:
                            wait_for(pe, y_done, U, item, -U)
                        if isinstance(item.n, int) and item.n == 0:
                            pe.wait_ge(w_lo, w2_chunks(f))
                        wait_for(pe, h_lo, FT, item, f + 1)
                        for u in range(U):
                            for m, (aa, aw) in enumerate(((0, 0), (0, 1), (1, 0))):
                                last = pe.matmul(acc[:, item.parity, u, :], hs[:, f % 4, aa, u * P:(u + 1) * P],
                                                 W2[:, aw, f, :], start=(f == 0 and m == 0),
                                                 stop=(f == FT - 1 and m == 2))
                        last.then_inc(ffn_done, 1)

            run_windows(pe, CHUNKS, emit, PEELED)


INPUTS = ["xT", "cT", "x", "Wq", "Wk", "Wv", "Wo", "W1", "W2", "bq", "bk", "bv", "b1",
          "bo", "g1", "be1", "b2", "g2", "be2"]


def build(nc, a, out):
    tokens, d = a["x"].shape
    ctx_rows = nc.dram_tensor("ctx_rows", [tokens, d], F32, kind="Internal").ap()
    attention(nc, a["xT"], a["cT"], {w: a["W" + w] for w in "vkq"}, {w: a["b" + w] for w in "kq"}, a["bv"], ctx_rows)
    feed(nc, ctx_rows, a["x"], a["Wo"], a["W1"], a["W2"], a["b1"],
         {v: a[v] for v in ("bo", "g1", "be1", "b2", "g2", "be2")}, out)


def kernel(**inputs):
    import concourse.bacc as bacc
    from concourse.bass_utils import run_bass_kernel_spmd

    def given(name):
        return np.asarray(inputs[name])

    def columns(v):
        return v.reshape(-1, P).T

    x, ctx = given("x"), given("ctx_1024")
    b, s, d = x.shape
    w = {n: given("L0_xattn_" + n) for n in ("Wq", "Wk", "Wv", "Wo", "W1", "W2", "bq", "bk", "bv", "bo", "b1", "b2",
                                             "ln1_g", "ln1_b", "ln2_g", "ln2_b")}
    layout = {"xT": x.transpose(0, 2, 1), "cT": ctx.transpose(0, 2, 1), "x": x.reshape(b * s, d),
              "Wq": w["Wq"], "Wk": w["Wk"], "Wv": w["Wv"], "Wo": w["Wo"], "W1": w["W1"], "W2": w["W2"],
              "bq": columns(w["bq"]), "bk": columns(w["bk"]), "bv": w["bv"], "b1": columns(w["b1"]),
              "bo": w["bo"], "g1": w["ln1_g"], "be1": w["ln1_b"], "b2": w["b2"], "g2": w["ln2_g"], "be2": w["ln2_b"]}
    nc = bacc.Bacc("TRN2", target_bir_lowering=False, num_devices=1, dynamic_dma_scratch_size=2048)
    arrays, args = {}, {}
    for name in INPUTS:
        arrays["in_" + name] = np.ascontiguousarray(layout[name])
        args[name] = nc.dram_tensor("in_" + name, arrays["in_" + name].shape, F32, kind="ExternalInput").ap()
    out = nc.dram_tensor("out", [b * s, d], F32, kind="ExternalOutput").ap()
    build(nc, args, out)
    result = run_bass_kernel_spmd(nc, [arrays], core_ids=[0])
    return result.results[0]["out"].reshape(b, s, d)
```

```python
import numpy as np

import concourse.bass as bass
from concourse import mybir
from contextlib import ExitStack

F32 = mybir.dt.float32
F32R = mybir.dt.float32r
BF16 = mybir.dt.bfloat16
U32 = mybir.dt.uint32
F16 = mybir.dt.float16
ALU = mybir.AluOpType
ACT = mybir.ActivationFunctionType
AX_X = mybir.AxisListType.X

P = 128
HEADS = 16
MASKED = -1e30
LN_EPS = 1e-5
PROB_BITS = 10
BACK = 2


class Item:

    def __init__(self, n, parity):
        self.n, self.parity = n, parity


def due(window, slot, slots, items, first, span=1):
    n, parity = window
    for back in range(BACK + 1):
        k = slot + slots * back - first
        if 0 <= k < span:
            at = n - back if back else n
            if not isinstance(at, int) or 0 <= at < items:
                yield Item(at, (parity - back) % 2), k


def after_first(steps):
    return [(item, k) for item, k in steps if not (isinstance(item.n, int) and item.n == 0)]


def wait_for(eng, sem, per, item, c):
    if isinstance(item.n, int):
        if per * item.n + c > 0:
            eng.wait_ge(sem, per * item.n + c)
    else:
        eng.wait_ge(sem, item.n * per + c if c else item.n * per)


def wait_for_all(eng, *waits):
    values = []
    for sem, per, item, c in waits:
        if isinstance(item.n, int):
            values.append(per * item.n + c)
        else:
            values.append(eng.snap(eng.to_reg(item.n * per + c)))
    for (sem, _, item, _), value in zip(waits, values):
        if not isinstance(item.n, int) or value > 0:
            eng.wait_ge(sem, value)


def run_windows(eng, items, emit, peeled=BACK):
    for w in range(peeled):
        emit((w, w % 2))
    with eng.Fori(0, (items - peeled) // 2) as pair:
        for parity in range(2):
            emit((pair * 2 + (peeled + parity), parity))
    for w in range(items, items + BACK):
        emit((w, w % 2))


def attention(nc, xT, cT, weights, biases, bv, ctx_rows, stored, load_early):
    B, D, S = xT.shape
    KT = D // P
    GROUPS = HEADS // 4
    HD = D // HEADS
    QT = S // P
    VW = 3 * HD + 2
    SLOTS = 12 * GROUPS
    SCALE = float(HD) ** -0.5
    PROB_BIAS = PROB_BITS * float(np.log(2.0))
    assert D == S == 512 and HD == 32 and B % 2 == 0 and B > BACK

    CTX_LOAD = 0
    CTX_SPLIT = 24
    X_LOAD = 28
    X_SPLIT = 37
    LIN = 32
    OUT = LIN + 4
    MAX_AT = LIN + 25
    ROW_AT = MAX_AT + 11
    ST_AT = ROW_AT + 6
    PV_AT = ST_AT + 3
    UNITS = [("v", 0), ("v", 1), ("k", 0), ("q", 0), ("v", 2), ("k", 1), ("q", 1), ("v", 3),
             ("k", 2), ("q", 2), ("k", 3), ("q", 3)]
    KQ_INDEX = {u: n for n, u in enumerate(u for u in UNITS if u[0] != "v")}
    GROUP_READY = {t: OUT + 4 * UNITS.index(("q", t)) + 1 for t in range(GROUPS)}
    EARLY = ROW_AT + 12 * (GROUPS - 1) + 1 - 2 * SLOTS
    MAX_UNITS = [(0, (0, 1, 2, 3)), (1, (0, 1)), (1, (2, 3)), (2, (0,)), (2, (1,)), (2, (2,)), (2, (3,)),
                 (3, (0,)), (3, (1,)), (3, (2,)), (3, (3,))]
    NMAX = len(MAX_UNITS)
    ST_UNITS = [((0, 0),), ((1, 0), (3, 3 * P)), ((2, 0),)]
    ST_WIDTH = [4 * P, 4 * P, 2 * P]
    FIRST = [("v", None), ("c", None), ("k", LIN + 1), ("q", LIN + 5)]
    NCHUNK = 2 * KT
    RAW = KT
    PROBS = 4

    with ExitStack() as stack:
        def sb(name, shape, dt):
            return stack.enter_context(nc.sbuf_tensor(name, shape, dt))

        def sem(name):
            return stack.enter_context(nc.semaphore(name))

        with ExitStack() as place:
            place.enter_context(nc.sbuf_tensor("first_at", [P, 4, KT, S], F32))
            first = place.enter_context(nc.sbuf_tensor("first", [P, len(FIRST), KT, S], F32))
        acts = {"c": sb("ctxT", [P, 2, KT, S], F32R), "x": sb("xT", [P, 2, KT, S], F32R)}
        stage = sb("stage", [P, 2, 2, 2, S], F32R)
        probs = sb("probs", [P, PROBS, S], F32)
        prob_hi = sb("prob_hi", [P, 4, S], F16)
        prob_lo = sb("prob_lo", [P, 4, S], F16)
        W = {w: sb(f"w{w}", [P, 2, KT, D], F32R) for w in "vkq"}
        heads = sb("heads", [P, GROUPS, 2, 4, S], F32R)
        raw = sb("raw", [P, RAW, D], F32)
        vf = sb("vf", [P, D], F32)
        V = sb("V", [P, 2, QT, HEADS, VW], BF16)
        maxima = sb("maxima", [P, 2, QT, 4], F32)
        negmax = sb("negmax", [P, QT, 4], F32)
        negmax_parts = sb("negmax_parts", [P, 2, 4, QT], F32)
        rows = sb("rows", [P, 2, 32], F32)
        osum = sb("osum", [P, QT, HD], F32)
        den = sb("den", [P, QT], F32)
        rden = sb("rden", [P, QT], F32)
        onorm = sb("onorm", [P, 2, QT, 4, HD], F32)
        bias = {"k": sb("bk", [P, GROUPS], F32), "q": sb("bq", [P, GROUPS], F32)}
        bvb = sb("bvb", [P, D], F32)
        identb = sb("identb", [P, P], BF16)
        mask_q = sb("mask_q", [P, S], BF16)
        mask_k = sb("mask_k", [P, 2, P], BF16)

        lin_ps = stack.enter_context(nc.psum_tensor("lin_ps", [P, 2, 512], F32))
        max_ps = stack.enter_context(nc.psum_tensor("max_ps", [P, 2, 512], F32))
        st_ps = stack.enter_context(nc.psum_tensor("st_ps", [P, 2, 512], F32))
        o_ps = stack.enter_context(nc.psum_tensor("o_ps", [P, 2, 512], F32))

        consts = sem("consts")
        const_loaded = sem("const_loaded")
        first_loaded = [sem(f"first_loaded{i}") for i in range(KT * len(FIRST))]
        raw_loaded = [sem(f"raw_loaded{i}") for i in range(RAW)]
        hi_done = sem("hi_done")
        lo_done = sem("lo_done")
        lin_step = sem("lin_step")
        kq_hi = sem("kq_hi")
        lin_out = sem("lin_out")
        v_hi = sem("v_hi")
        v_rest = sem("v_rest")
        v_mid = sem("v_mid")
        v_lo = sem("v_lo")
        heads_loaded = [sem(f"heads_loaded{t}") for t in range(GROUPS)]
        max_done = sem("max_done")
        max_passed = sem("max_passed")
        max_read = sem("max_read")
        neg_step = sem("neg_step")
        rows_ready = sem("rows_ready")
        rows_loaded = [sem(f"rows_loaded{i}") for i in range(2)]
        st_done = sem("st_done")
        exp_done = sem("exp_done")
        pl_done = sem("pl_done")
        pv_done = sem("pv_done")
        o_step = sem("o_step")
        o_read = sem("o_read")
        o_out = sem("o_out")

        def chunk_of(kind, j):
            return {"c": 3 * KT, "x": 4 * KT}[kind] + j

        firsts = {"v": W["v"], "c": acts["c"], "k": W["k"], "q": W["q"]}

        def first_split(kind, split_chunk):
            g = [f for f, _ in FIRST].index(kind)
            for j in range(KT):
                split_chunk(g * KT + j, first[:, g, j, :], firsts[kind][:, :, j, :])

        block = stack.enter_context(nc.Block())

        @block.sync
        def _(sp):
            sources = {"v": weights["v"], "c": cT[0], "k": weights["k"], "q": weights["q"]}
            for g, (kind, _) in enumerate(FIRST):
                for j in range(KT):
                    sp.dma_start(first[:, g, j, :], sources[kind][j * P:(j + 1) * P, :]
                                 ).then_inc(first_loaded[g * KT + j], 16)
                if kind == "c":
                    for w in "kq":
                        sp.dma_start(bias[w][:, :], biases[w]).then_inc(const_loaded, 16)
                    sp.dma_start(bvb[:, :], bv.rearrange("(a n) -> a n", a=1).to_broadcast([P, D])
                                 ).then_inc(const_loaded, 16)
                if kind == "k":
                    for i in range(KT):
                        sp.dma_start(raw[:, i, :], xT[0, i * P:(i + 1) * P, :]).then_inc(raw_loaded[i], 16)

            def source(a, item, j):
                if isinstance(item.n, int):
                    return a[item.n, j * P:(j + 1) * P, :]
                return a[bass.ds(sp.snap(item.n), 1), j * P:(j + 1) * P, :].rearrange("a p s -> (a p) s")

            def emit(window):
                for s in range(SLOTS):
                    if isinstance(window[0], int) and (window[0], s) == (B + 1, EARLY):
                        sp.wait_ge(lin_step, SLOTS * B)
                        for i in range(2):
                            sp.wait_ge(stored[i], 16 * GROUPS // 2)
                        load_early(sp)
                    for t in range(GROUPS):
                        for item, _ in due(window, s, SLOTS, B, GROUP_READY[t]):
                            wait_for_all(sp, (lin_out, len(UNITS), item, UNITS.index(("q", t)) + 1),
                                         (st_done, SLOTS, item, 12 * t + 12 - SLOTS))
                            for part in range(3):
                                for i in range(4):
                                    four = stage[32 * i:32 * i + 32, t % 2, :, :, :].rearrange("p a b n -> p (a b) n")
                                    pick = (four[:, 0:3:2, :], four[:, 1:3, :], four[:, 0:4:3, :])[part]
                                    sp.dma_start(heads[32 * part:32 * part + 32, t, :, i, :].bitcast(F32),
                                                 pick.bitcast(F32)).then_inc(heads_loaded[t], 16)
                    for j in range(KT):
                        for item, _ in after_first(due(window, s, SLOTS, B, CTX_LOAD + 2 * j)):
                            src = source(cT, item, j)
                            wait_for_all(sp, (lo_done, NCHUNK, item, chunk_of("x", j) + 1 - NCHUNK))
                            sp.dma_start(raw[:, j, :], src).then_inc(raw_loaded[j], 16)
                        for item, _ in after_first(due(window, s, SLOTS, B, X_LOAD + 2 * j)):
                            src = source(xT, item, j)
                            wait_for_all(sp, (lo_done, NCHUNK, item, chunk_of("c", j) + 1))
                            sp.dma_start(raw[:, j, :], src).then_inc(raw_loaded[j], 16)
                    for t in range(GROUPS):
                        for item, _ in due(window, s, SLOTS, B, PV_AT + 12 * t + 14):
                            f = t * P
                            if isinstance(item.n, int):
                                dst = ctx_rows[item.n * S:(item.n + 1) * S, f:f + P]
                            else:
                                dst = ctx_rows[bass.ds(sp.snap(item.n * S), S), f:f + P]
                            wait_for_all(sp, (o_out, HEADS, item, 4 * t + 4))
                            sp.dma_start(dst.rearrange("(q p) n -> p q n", p=P),
                                         onorm[:, t % 2, :, :, :].rearrange("p q h d -> p q (h d)")
                                         ).then_inc(stored[t % 2], 16)
                    for t in range(GROUPS):
                        for item, _ in due(window, s, SLOTS, B, ROW_AT + 12 * t):
                            wait_for_all(sp, (rows_ready, GROUPS, item, t + 1))
                            both = heads[96:98, t, 0, :, :].bitcast(F32).rearrange("p h (q a n) -> p (h q) a n",
                                                                                   a=P // 32, n=32)
                            for a in range(P // 32):
                                sp.dma_start(both[:, :, a, :], rows[32 * a:32 * a + 32, t % 2, :]
                                             ).then_inc(rows_loaded[t % 2], 16)

            run_windows(sp, B, emit)

        @block.gpsimd
        def _(pool):
            zeros = vf[:, 0:P // 2].bitcast(BF16)
            pool.memset(vf[:, 0:P // 2], 0.0).then_inc(consts, 1)
            pool.wait_ge(consts, 1)
            pool.memset(heads[96:98, :, 1, :, :].bitcast(F32), 1.0).then_inc(consts, 1)
            pool.wait_ge(consts, 2)
            pool.memset(V[:, :, :, :, 3 * HD:VW], 1.0).then_inc(consts, 1)
            pool.wait_ge(consts, 3)
            pool.affine_select(out=identb[:, :], in_=zeros, compare_op=ALU.not_equal, fill=1.0,
                               base=0, pattern=[[-1, P]], channel_multiplier=1).then_inc(consts, 1)
            pool.memset(mask_q[:, 0:S - P], 0.0).then_inc(consts, 1)
            pool.affine_select(out=mask_q[:, S - P:S], in_=zeros, compare_op=ALU.is_gt, fill=MASKED,
                               base=0, pattern=[[-1, P]], channel_multiplier=1).then_inc(consts, 1)
            for i in range(2):
                pool.affine_select(out=mask_k[:, i, :], in_=zeros, compare_op=ALU.is_gt, fill=MASKED,
                                   base=0, pattern=[[1, P]], channel_multiplier=-1).then_inc(consts, 1)

            def emit(window):
                for s in range(SLOTS):
                    for item, k in due(window, s, SLOTS, B, ST_AT, SLOTS):
                        w = ST_WIDTH[k % 3]
                        wait_for(pool, exp_done, SLOTS, item, k + 1)
                        wait_for(pool, pv_done, SLOTS, item, k + 1 - 4)
                        pool.tensor_tensor(prob_lo[:, k % 4, 0:w], probs[:, k % PROBS, 0:w],
                                           prob_hi[:, k % 4, 0:w], ALU.subtract).then_inc(pl_done, 1)

            run_windows(pool, B, emit)

        @block.scalar
        def _(act):
            def split(item, kind, j):
                wait_for(act, raw_loaded[j], 32, item, 16 if kind == "x" else 0)
                act.activation(acts[kind][:, 0, j, :], raw[:, j, :], ACT.Copy).then_inc(hi_done, 1)

            def split_first(n, src, parts):
                act.wait_ge(first_loaded[n], 16)
                act.activation(parts[:, 0, :], src, ACT.Copy).then_inc(hi_done, 1)

            for kind, at in FIRST:
                if at is None:
                    first_split(kind, split_first)
            act.wait_ge(const_loaded, 48)

            def emit(window):
                for s in range(SLOTS):
                    for kind, at in FIRST:
                        if isinstance(window[0], int) and (window[0], s) == (0, at):
                            first_split(kind, split_first)
                    for n, (kind, t) in enumerate(UNITS):
                        if kind == "v":
                            for item, _ in due(window, s, SLOTS, B, OUT + 4 * n + 1):
                                wait_for(act, lin_out, len(UNITS), item, n + 1)
                                wait_for(act, pv_done, SLOTS, item, 1 - SLOTS)
                                act.activation(V[:, item.parity, t, :, HD:2 * HD],
                                               vf[:, :].rearrange("p (h d) -> p h d", d=HD), ACT.Copy
                                               ).then_inc(v_hi, 1)
                            for item, _ in due(window, s, SLOTS, B, OUT + 4 * n + 3):
                                wait_for(act, v_rest, QT, item, t + 1)
                                act.activation(V[:, item.parity, t, :, 2 * HD:3 * HD],
                                               vf[:, :].rearrange("p (h d) -> p h d", d=HD), ACT.Copy
                                               ).then_inc(v_mid, 1)
                        else:
                            for item, _ in due(window, s, SLOTS, B, OUT + 4 * n):
                                wait_for(act, lin_step, SLOTS, item, 4 * n + 4)
                                wait_for(act, heads_loaded[(t - 2) % GROUPS], 192, item, 192 if t > 1 else 0)
                                act.activation(stage[:, t % 2, "qk".index(kind), 0, :], lin_ps[:, n % 2, :],
                                               ACT.Identity, bias=bias[kind][:, t:t + 1]).then_inc(kq_hi, 1)
                    for j in range(KT):
                        for item, _ in after_first(due(window, s, SLOTS, B, CTX_SPLIT + 2 * j)):
                            wait_for(act, lin_step, SLOTS, item, 4 * UNITS.index(("k", 3)) + j + 1 - SLOTS)
                            split(item, "c", j)
                        for item, _ in due(window, s, SLOTS, B, X_SPLIT + 2 * j):
                            wait_for(act, lin_step, SLOTS, item, 4 * UNITS.index(("q", 3)) + j + 1 - SLOTS)
                            split(item, "x", j)
                    for item, k in due(window, s, SLOTS, B, ST_AT, SLOTS):
                        w = ST_WIDTH[k % 3]
                        wait_for(act, st_done, SLOTS, item, k + 1)
                        wait_for(act, pl_done, SLOTS, item, k + 1 - PROBS)
                        wait_for(act, pv_done, SLOTS, item, k + 1 - 4)
                        act.activation(probs[:, k % PROBS, 0:w], st_ps[:, k % 2, 0:w], ACT.Exp, bias=PROB_BIAS,
                                       scale=SCALE)
                        act.activation(prob_hi[:, k % 4, 0:w], st_ps[:, k % 2, 0:w], ACT.Exp, bias=PROB_BIAS,
                                       scale=SCALE
                                       ).then_inc(exp_done, 1)

            run_windows(act, B, emit)

        @block.vector
        def _(dve):
            def split(item, kind, j):
                wait_for(dve, hi_done, NCHUNK, item, chunk_of(kind, j) + 1)
                dve.tensor_tensor(acts[kind][:, 1, j, :], raw[:, j, :], acts[kind][:, 0, j, :], ALU.subtract
                                  ).then_inc(lo_done, 1)

            def split_first(n, src, parts):
                dve.wait_ge(hi_done, n + 1)
                dve.tensor_tensor(parts[:, 1, :], src, parts[:, 0, :], ALU.subtract).then_inc(lo_done, 1)

            for kind, at in FIRST:
                if at is None:
                    first_split(kind, split_first)
            dve.wait_ge(const_loaded, 48)

            def emit(window):
                for s in range(SLOTS):
                    for kind, at in FIRST:
                        if isinstance(window[0], int) and (window[0], s) == (0, at):
                            first_split(kind, split_first)
                    for t in range(GROUPS):
                        for item, _ in due(window, s, SLOTS, B, ROW_AT + 12 * t):
                            wait_for(dve, max_read, NMAX * GROUPS, item, NMAX * (t + 1))
                            wait_for(dve, rows_ready, GROUPS, item, t)
                            dve.tensor_scalar(negmax[:, :, :], maxima[:, t % 2, :, :], -1e28, -1.0, ALU.max, ALU.mult
                                              ).then_inc(neg_step, 1)
                            wait_for(dve, neg_step, 3 * GROUPS, item, 3 * t + 1)
                            by_head = negmax[:, :, :].rearrange("p q h -> p h q")
                            hi, lo = negmax_parts[:, 0, :, :], negmax_parts[:, 1, :, :]
                            dve.tensor_copy(hi.bitcast(F32R), by_head).then_inc(neg_step, 1)
                            wait_for(dve, neg_step, 3 * GROUPS, item, 3 * t + 2)
                            dve.tensor_tensor(lo.bitcast(F32R), by_head, hi, ALU.subtract).then_inc(neg_step, 1)
                            wait_for(dve, neg_step, 3 * GROUPS, item, 3 * t + 3)
                            wait_for(dve, rows_loaded[t % 2], 128, item, 64 * (t // 2))
                            dve.transpose(rows[:, t % 2, :].bitcast(U32),
                                          negmax_parts[:, :, :, :].rearrange("p c h q -> p (c h q)").bitcast(U32)
                                          ).then_inc(rows_ready, 1)
                    for j in range(KT):
                        for item, _ in after_first(due(window, s, SLOTS, B, CTX_SPLIT + 2 * j + 2)):
                            split(item, "c", j)
                        for item, _ in due(window, s, SLOTS, B, X_SPLIT + 2 * j + 2):
                            split(item, "x", j)
                    for n, (kind, t) in enumerate(UNITS):
                        if kind == "v":
                            for item, _ in due(window, s, SLOTS, B, OUT + 4 * n):
                                wait_for(dve, lin_step, SLOTS, item, 4 * n + 4)
                                wait_for(dve, v_lo, QT, item, t)
                                dve.tensor_tensor(vf[:, :], lin_ps[:, n % 2, :], bvb[:, :], ALU.add
                                                  ).then_inc(lin_out, 1)
                            vr = vf[:, :].rearrange("p (h d) -> p h d", d=HD)
                            for item, _ in due(window, s, SLOTS, B, OUT + 4 * n + 2):
                                wait_for(dve, v_hi, QT, item, t + 1)
                                dve.tensor_tensor(vr, vr, V[:, item.parity, t, :, HD:2 * HD], ALU.subtract
                                                  ).then_inc(v_rest, 1)
                            for item, _ in due(window, s, SLOTS, B, OUT + 4 * n + 3):
                                wait_for(dve, v_mid, QT, item, t + 1)
                                dve.tensor_tensor(V[:, item.parity, t, :, 0:HD], vr,
                                                  V[:, item.parity, t, :, 2 * HD:3 * HD], ALU.subtract
                                                  ).then_inc(v_lo, 1)
                        else:
                            qk = "qk".index(kind)
                            for item, _ in due(window, s, SLOTS, B, OUT + 4 * n):
                                wait_for(dve, kq_hi, len(KQ_INDEX), item, KQ_INDEX[kind, t] + 1)
                                dve.scalar_tensor_tensor(out=stage[:, t % 2, qk, 1, :], in0=lin_ps[:, n % 2, :],
                                                         scalar=bias[kind][:, t:t + 1], in1=stage[:, t % 2, qk, 0, :],
                                                         op0=ALU.add, op1=ALU.subtract).then_inc(lin_out, 1)
                    for t in range(GROUPS):
                        for item, k in due(window, s, SLOTS, B, MAX_AT + 12 * t, 12):
                            if k < NMAX:
                                q, hs = MAX_UNITS[k]
                                n = NMAX * t + k
                                if k == 0:
                                    wait_for(dve, rows_ready, GROUPS, item, t - 1)
                                wait_for(dve, max_done, NMAX * GROUPS, item, n + 1)
                                dve.sem_inc(max_passed, 1)
                                w = P * (q + 1)
                                for a, h in enumerate(hs):
                                    scores = max_ps[:, (MAX_AT + 12 * t + k) % 2, a * w:(a + 1) * w]
                                    last = dve.tensor_tensor_reduce(
                                        out=scores, in0=scores,
                                        in1=mask_q[:, S - w:S], scale=1.0, scalar=MASKED, op0=ALU.add, op1=ALU.max,
                                        accum_out=maxima[:, t % 2, q, h:h + 1])
                                last.then_inc(max_read, 1)
                    for h in range(HEADS):
                        t, i = h // 4, h % 4
                        o = o_ps[:, h % 2, 0:QT * VW].rearrange("p (q w) -> p q w", w=VW)
                        for item, _ in due(window, s, SLOTS, B, PV_AT + 3 * h + 3):
                            wait_for(dve, pv_done, SLOTS, item, 3 * h + 3)
                            wait_for(dve, o_out, HEADS, item, h)
                            dve.tensor_scalar(den[:, :], o[:, :, 3 * HD], 1e-30, None, ALU.max).then_inc(o_step, 1)
                            dve.tensor_reduce(osum[:, :, :],
                                              o[:, :, 0:3 * HD].rearrange("p q (c d) -> p q d c", c=3),
                                              AX_X, ALU.add).then_inc(o_read, 1)
                            wait_for(dve, o_step, 2 * HEADS, item, 2 * h + 1)
                            dve.reciprocal(rden[:, :], den[:, :]).then_inc(o_step, 1)
                        for item, _ in due(window, s, SLOTS, B, PV_AT + 3 * h + 4):
                            wait_for(dve, o_read, HEADS, item, h + 1)
                            wait_for(dve, o_step, 2 * HEADS, item, 2 * h + 2)
                            if i == 0:
                                wait_for(dve, stored[t % 2], 32, item, 16 * (t // 2))
                            dve.tensor_tensor(onorm[:, t % 2, :, i, :], osum[:, :, :],
                                              rden[:, :].unsqueeze(2).to_broadcast([P, QT, HD]), ALU.mult
                                              ).then_inc(o_out, 1)

            run_windows(dve, B, emit)

        @block.tensor
        def _(pe):
            pe.wait_ge(consts, 8)

            def scores_for_max(item, t, k):
                q, hs = MAX_UNITS[k]
                bank = (MAX_AT + 12 * t + k) % 2
                n = NMAX * t + k
                if k == 0:
                    wait_for(pe, heads_loaded[t], 192, item, 192)
                wait_for(pe, max_read, NMAX * GROUPS, item, (n, n - 2)[k] if k < 2 else n - 1)
                w = P * (q + 1)
                for a, i in enumerate(hs):
                    last = pe.matmul(max_ps[:, bank, a * w:(a + 1) * w], heads[0:96, t, 0, i, q * P:(q + 1) * P],
                                     heads[0:96, t, 1, i, 0:w], start=(a == 0), stop=(a == len(hs) - 1),
                                     skip_group_check=True)
                last.then_inc(max_done, 1)

            def linear(window, s):
                for n, (kind, t) in enumerate(UNITS):
                    a = acts["x" if kind == "q" else "c"]
                    for item, j in due(window, s, SLOTS, B, LIN + 4 * n, 4):
                        first = isinstance(item.n, int) and item.n == 0
                        if n == 0 and first:
                            pe.wait_ge(lo_done, KT + j + 1)
                        elif n in (0, UNITS.index(("q", 0))):
                            wait_for(pe, lo_done, NCHUNK, item, chunk_of("cx"[n > 0], j) + 1)
                        elif first and (kind, t) == ("k", 0) and j == 0:
                            pe.wait_ge(lo_done, 3 * KT)
                        if j == 0:
                            wait_for(pe, lin_out, len(UNITS), item, n - 1)
                        for m, (aw, aa) in enumerate(((0, 0), (0, 1), (1, 0))):
                            if kind == "v":
                                last = pe.matmul(lin_ps[:, n % 2, :], a[:, aw, j, t * P:(t + 1) * P],
                                                 W[kind][:, aa, j, :], start=(j == 0 and m == 0),
                                                 stop=(j == KT - 1 and m == 2))
                            else:
                                last = pe.matmul(lin_ps[:, n % 2, :], W[kind][:, aw, j, t * P:(t + 1) * P],
                                                 a[:, aa, j, :], start=(j == 0 and m == 0),
                                                 stop=(j == KT - 1 and m == 2))
                        last.then_inc(lin_step, 1)

            def maximum_scores(window, s):
                for t in range(GROUPS):
                    for item, k in due(window, s, SLOTS, B, MAX_AT + 12 * t, 12):
                        if k < NMAX:
                            scores_for_max(item, t, k)

            def transposed_scores(window, s, opens):
                for item, k in due(window, s, SLOTS, B, ST_AT, SLOTS):
                    t, i, c = k // 12, k // 3 % 4, k % 3
                    if k % 12 == 0:
                        wait_for(pe, rows_loaded[t % 2], 128, item, 64 * (t // 2 + 1))
                    if opens:
                        wait_for(pe, exp_done, SLOTS, item, k + 1 - 2)
                    for m, (kt, at) in enumerate(ST_UNITS[c]):
                        w = S - kt * P
                        last = pe.matmul(st_ps[:, k % 2, at:at + w], heads[0:98, t, 1, i, kt * P:(kt + 1) * P],
                                         heads[0:98, t, 0, i, kt * P:S], start=(opens and m == 0), stop=not opens,
                                         skip_group_check=True)
                    if not opens:
                        last.then_inc(st_done, 1)

            def values(window, s):
                for item, k in due(window, s, SLOTS, B, PV_AT, SLOTS):
                    h, c = k // 3, k % 3
                    if k == 0:
                        wait_for(pe, v_lo, QT, item, QT)
                    if c == 0:
                        wait_for(pe, o_read, HEADS, item, h - 1)
                    wait_for(pe, pl_done, SLOTS, item, k + 1)
                    for m, (kt, at) in enumerate(ST_UNITS[c]):
                        for q in range(kt, QT):
                            col = at + (q - kt) * P
                            o = o_ps[:, h % 2, q * VW:(q + 1) * VW]
                            v = V[:, item.parity, kt, h, :]
                            pe.matmul(o[:, 0:3 * HD + 1], prob_hi[:, k % 4, col:col + P], v[:, 0:3 * HD + 1],
                                      start=(k % 3 == 0 and q == 0), stop=False, skip_group_check=True)
                            last = pe.matmul(o[:, HD:3 * HD + 1], prob_lo[:, k % 4, col:col + P],
                                             v[:, HD:3 * HD + 1], start=False, stop=(c == 2),
                                             skip_group_check=True)
                    last.then_inc(pv_done, 1)

            def masks(window, s, opens):
                for item, k in due(window, s, SLOTS, B, ST_AT, SLOTS):
                    unit = ST_UNITS[k % 3]
                    tiles = st_ps[:, k % 2, :].rearrange("p (c n) -> p c n", n=P)[:, 0:KT:unit[-1][1] // P or KT, :]
                    if opens:
                        wait_for(pe, exp_done, SLOTS, item, k + 1 - 2)
                    last = pe.matmul(tiles, identb[:, :], mask_k[:, 0:len(unit), :], start=opens, stop=not opens,
                                     skip_group_check=True)
                    if not opens:
                        last.then_inc(st_done, 1)

            def emit(window):
                for s in range(SLOTS):
                    if s % 2 == 0:
                        linear(window, s)
                        maximum_scores(window, s)
                        transposed_scores(window, s, True)
                        masks(window, s, False)
                        values(window, s)
                    else:
                        values(window, s)
                        masks(window, s, True)
                        transposed_scores(window, s, False)
                        linear(window, s)
                        maximum_scores(window, s)

            run_windows(pe, B, emit)

        return 16 * B * GROUPS // 2


FRONT_VECTORS = ("bo", "g1", "be1")
BACK_VECTORS = ("b2", "g2", "be2")


class Early:

    def __init__(self, nc, stack, d, ff):
        self.RAW, self.U, self.bytes = 4, 2, 0
        with ExitStack() as place:
            def sb(name, shape):
                self.bytes += 4 * int(np.prod(shape[1:]))
                return place.enter_context(nc.sbuf_tensor(name, shape, F32))

            self.raw = sb("raw2", [P, self.RAW, d])
            self.o_in = sb("o_in", [P, self.U, d])
            self.x_in = sb("x_in", [P, self.U, d])
            self.vec = {v: sb("vec_" + v, [P, d]) for v in FRONT_VECTORS + BACK_VECTORS}
            self.b1c = sb("b1c", [P, ff // P])
        self.stored = [stack.enter_context(nc.semaphore(f"stored{i}")) for i in range(2)]
        self.raw_loaded = [stack.enter_context(nc.semaphore(f"w_loaded{i}")) for i in range(self.RAW)]
        self.o_loaded = [stack.enter_context(nc.semaphore(f"o_loaded{u}")) for u in range(self.U)]
        self.x_loaded = stack.enter_context(nc.semaphore("x_loaded"))
        self.front_loaded = stack.enter_context(nc.semaphore("front_loaded"))
        self.back_loaded = stack.enter_context(nc.semaphore("back_loaded"))

    def load_blocks(self, sp, u, rows, loaded):
        for b in range(P // 32):
            src = rows.rearrange("(a t) (j b f) -> b t j a f", t=32, f=32, b=P // 32)[b]
            dst = self.o_in[32 * b:32 * b + 32, u, :].rearrange("t (j a f) -> t j a f", f=32, a=P // 32)
            sp.dma_start(dst, src).then_inc(loaded[u], 16)

    def load_tokens(self, sp, ctx_rows, x):
        for u in range(self.U):
            self.load_blocks(sp, u, ctx_rows[u * P:(u + 1) * P, :], self.o_loaded)
        sp.dma_start(self.x_in[:, :, :], x.rearrange("(u p) n -> p u n", p=P)).then_inc(self.x_loaded, 16)

    def load(self, sp, ctx_rows, x, wo, b1, vectors):
        T = self.U * P
        self.load_tokens(sp, ctx_rows[0:T, :], x[0:T, :])
        for n in range(self.RAW):
            sp.dma_start(self.raw[:, n, :], wo[n * P:(n + 1) * P, :]).then_inc(self.raw_loaded[n], 16)
        for names, loaded in ((FRONT_VECTORS, self.front_loaded), (BACK_VECTORS, self.back_loaded)):
            for v in names:
                sp.dma_start(self.vec[v][:, :], vectors[v].rearrange("(a n) -> a n", a=1).to_broadcast([P, x.shape[1]])
                             ).then_inc(loaded, 16)
        sp.dma_start(self.b1c[:, :], b1).then_inc(self.front_loaded, 16)


def feed(nc, ctx_rows, all_stored, x, wo, w1, w2, early, out):
    N, D = x.shape
    FF = w1.shape[1]
    KT, FT = D // P, FF // P
    U = early.U
    T = U * P
    CHUNKS = N // T
    SLOTS = FT
    assert early.RAW == KT
    assert D == 512 and FT == 16 and N % T == 0 and CHUNKS % 2 == 0 and CHUNKS > BACK

    LOAD = 0
    ADD_BO = 2
    OTR = 2
    PROJ = 5
    RES = 7
    NORM1 = 10
    X1_TURN = 14
    FFN1 = 16
    FFN2 = FFN1 + 2
    RES2 = FFN2 + FT
    STORE = RES2 + 4
    W1Q = FF // 512
    RAW = early.RAW
    PEELED = 4

    with ExitStack() as stack:
        def sb(name, shape, dt):
            return stack.enter_context(nc.sbuf_tensor(name, shape, dt))

        def sem(name):
            return stack.enter_context(nc.semaphore(name))

        sb("early", [P, early.bytes], mybir.dt.uint8)
        raw, o_in, x_in, vec, b1c = early.raw, early.o_in, early.x_in, early.vec, early.b1c
        raw_loaded, o_loaded, x_loaded = early.raw_loaded, early.o_loaded, early.x_loaded
        front_loaded, back_loaded = early.front_loaded, early.back_loaded
        x1_rows = nc.dram_tensor("x1_rows", [T, D], F32, kind="Internal").ap()
        Wo = sb("Wo", [P, 2, KT, D], F32R)
        W1 = sb("W1", [P, 2, KT, FF], F32R)
        W2 = sb("W2", [P, 2, FT, D], F32R)
        turned = sb("turned", [P, 2, 2, KT, T], F32R)
        block_turned = sb("block_turned", [P, KT, P], F32)
        x1 = sb("x1", [P, 2, U, D], F32)
        hf = sb("hf", [P, 2, T], F32)
        hs = sb("hs", [P, 4, 2, T], F32R)
        y = sb("y", [P, U, D], F32)
        stats = sb("stats", [P, 2, U, 6], F32)
        mv = sb("mv", [P, 2, U, 2], F32)
        gate = sb("gate", [P, 2, 1], F32)
        sd = sb("sd", [P, 2, U], F32)
        ve = sb("ve", [P, 2, U], F32)
        rs = sb("rs", [P, 2, 3, U], F32)

        acc = stack.enter_context(nc.psum_tensor("acc", [P, 2, U, 512], F32))
        h_ps = stack.enter_context(nc.psum_tensor("h_ps", [P, 2, 512], F32))
        front = stack.enter_context(nc.psum_tensor("front", [P, 2, 512], F32))

        w_hi = sem("w_hi")
        w_lo = sem("w_lo")
        bo_added = sem("bo_added")
        ctx_turned = sem("ctx_turned")
        x1_stored = [sem(f"x1_stored{u}") for u in range(U)]
        x1_loaded = [sem(f"x1_loaded{u}") for u in range(U)]
        x1_turned = sem("x1_turned")
        turned_hi = sem("turned_hi")
        turned_lo = sem("turned_lo")
        proj_done = sem("proj_done")
        res_done = sem("res_done")
        ln_step = [sem("ln1_step"), sem("ln2_step")]
        ln_root = [sem("ln1_root"), sem("ln2_root")]
        ln_var = [sem("ln1_var"), sem("ln2_var")]
        ln_sd = [sem("ln1_sd"), sem("ln2_sd")]
        ln_scaled = [sem("ln1_scaled"), sem("ln2_scaled")]
        ln_out = [sem("ln1_out"), sem("ln2_out")]
        b2_added = sem("b2_added")
        h_done = sem("h_done")
        h_out = sem("h_out")
        h_lo = sem("h_lo")
        ffn_done = sem("ffn_done")
        y_done = sem("y_done")
        y_stored = sem("y_stored")

        chunks = [(wo.rearrange("(k p) n -> k p n", p=P)[j], Wo[:, :, j, :]) for j in range(KT)]
        for q in range(W1Q):
            chunks += [(w1[j * P:(j + 1) * P, q * 512:(q + 1) * 512], W1[:, :, j, q * 512:(q + 1) * 512])
                       for j in range(KT)]
            chunks += [(w2.rearrange("(k p) n -> k p n", p=P)[f], W2[:, :, f, :])
                       for f in range(q * FT // W1Q, (q + 1) * FT // W1Q)]

        def w1_chunks(f):
            q = f // (FT // W1Q)
            return KT + q * (KT + FT // W1Q) + KT

        def w2_chunks(f):
            return w1_chunks(f) + f % (FT // W1Q) + 1

        def split_slot(n):
            return OTR + 1 if n < KT else PROJ + (n - KT) * 3 // 4

        def weights_due(window, slot):
            if isinstance(window[0], int) and window[0] < BACK:
                return [n for n in range(len(chunks)) if split_slot(n) == slot + SLOTS * window[0]]
            return []

        LNS = 2 * U + 5

        block = stack.enter_context(nc.Block())

        @block.sync
        def _(sp):
            for i in range(2):
                sp.wait_ge(early.stored[i], all_stored)

            def token_rows(a, item):
                if isinstance(item.n, int):
                    return a[item.n * T:(item.n + 1) * T, :]
                return a[bass.ds(sp.snap(item.n * T), T), :]

            def emit(window):
                for s in range(SLOTS):
                    for item, _ in after_first(due(window, s, SLOTS, CHUNKS, LOAD)):
                        src_o, src_x = token_rows(ctx_rows, item), token_rows(x, item)
                        wait_for_all(sp, (x1_turned, U, item, 0), (res_done, U, item, 0))
                        early.load_tokens(sp, src_o, src_x)
                    for item, _ in due(window, s, SLOTS, CHUNKS, NORM1 + 1):
                        for u in range(U):
                            wait_for_all(sp, (ln_out[0], U, item, u + 1))
                            sp.dma_start(x1_rows[u * P:(u + 1) * P, :], x1[:, item.parity, u, :]
                                         ).then_inc(x1_stored[u], 16)
                        for u in range(U):
                            wait_for_all(sp, (x1_stored[u], 16, item, 16), (ctx_turned, U, item, U))
                            early.load_blocks(sp, u, x1_rows[u * P:(u + 1) * P, :], x1_loaded)
                    for n in weights_due(window, s):
                        if n + RAW < len(chunks):
                            sp.wait_ge(w_lo, n + 1)
                            sp.dma_start(raw[:, n % RAW, :], chunks[n + RAW][0]).then_inc(raw_loaded[n % RAW], 16)
                    for item, _ in due(window, s, SLOTS, CHUNKS, STORE):
                        dst = token_rows(out, item).rearrange("(u p) n -> p u n", p=P)
                        wait_for_all(sp, (ln_out[1], U, item, U))
                        sp.dma_start(dst, y[:, :, :]).then_inc(y_stored, 16)

            run_windows(sp, CHUNKS, emit, PEELED)
            sp.wait_ge(y_stored, 16 * CHUNKS)

        @block.gpsimd
        def _(pool):
            pool.wait_ge(front_loaded, 16 * (len(FRONT_VECTORS) + 1))

            def emit(window):
                for s in range(SLOTS):
                    for u in range(U):
                        for item, _ in due(window, s, SLOTS, CHUNKS, ADD_BO + u):
                            wait_for(pool, x_loaded, 16, item, 16)
                            pool.tensor_tensor(x_in[:, u, :], x_in[:, u, :], vec["bo"][:, :], ALU.add
                                               ).then_inc(bo_added, 1)
                        for item, _ in due(window, s, SLOTS, CHUNKS, X1_TURN + u):
                            wait_for(pool, x1_stored[u], 16, item, 16)
                            if isinstance(item.n, int) and item.n == 0:
                                pool.wait_ge(back_loaded, 16 * len(BACK_VECTORS))
                            t = x1[:, item.parity, u, :]
                            pool.tensor_tensor(t, t, vec["b2"][:, :], ALU.add).then_inc(b2_added, 1)

            run_windows(pool, CHUNKS, emit, PEELED)

        @block.scalar
        def _(act):
            def root(norm, item):
                wait_for(act, ln_var[norm], 1, item, 1)
                act.activation(sd[:, norm, :], ve[:, norm, :], ACT.Sqrt).then_inc(ln_sd[norm], 1)

            def emit(window):
                for s in range(SLOTS):
                    for kind, at in ((0, OTR), (1, X1_TURN)):
                        for u in range(U):
                            for item, _ in due(window, s, SLOTS, CHUNKS, at + (1 + 2 * u, u)[kind]):
                                n = U * kind + u
                                both = turned[:, item.parity, :, :, u * P:(u + 1) * P]
                                if kind:
                                    wait_for(act, x1_turned, U, item, u + 1)
                                    wait_for(act, proj_done, U, item, U)
                                else:
                                    wait_for(act, ctx_turned, U, item, u + 1)
                                    wait_for(act, h_done, FT, item, -FT)
                                act.activation(both[:, 0, :, :], block_turned[:, :, :], ACT.Copy).then_inc(turned_hi, 1)
                    for n in weights_due(window, s):
                        act.wait_ge(raw_loaded[n % RAW], 16 * (n // RAW + 1))
                        act.activation(chunks[n][1][:, 0, :], raw[:, n % RAW, :], ACT.Copy).then_inc(w_hi, 1)
                    for item, _ in due(window, s, SLOTS, CHUNKS, NORM1):
                        root(0, item)
                    for item, _ in due(window, s, SLOTS, CHUNKS, RES2 + 1):
                        root(1, item)
                    for item, f in due(window, s, SLOTS, CHUNKS, FFN1, FT):
                        if isinstance(item.n, int) and item.n == 0 and f == 0:
                            act.wait_ge(front_loaded, 16 * (len(FRONT_VECTORS) + 1))
                        wait_for(act, h_done, FT, item, f + 1)
                        wait_for(act, h_lo, FT, item, f + 1 - 2)
                        wait_for(act, ffn_done, FT, item, f + 1 - 4)
                        act.activation(hf[:, f % 2, :], h_ps[:, f % 2, 0:T], ACT.Relu,
                                       bias=b1c[:, f:f + 1])
                        act.activation(hs[:, f % 4, 0, :], h_ps[:, f % 2, 0:T], ACT.Relu,
                                       bias=b1c[:, f:f + 1]).then_inc(h_out, 1)

            run_windows(act, CHUNKS, emit, PEELED)

        @block.vector
        def _(dve):
            def statistics(norm, item, u, tile):
                dve.bn_stats(stats[:, norm, u, :], tile).then_inc(ln_step[norm], 1)

            def variance(norm, item, tiles):
                wait_for(dve, ln_step[norm], LNS, item, U)
                dve.tensor_copy(gate[:, norm, :], stats[:, norm, 0, 0:1]).then_inc(ln_step[norm], 1)
                for u in range(U):
                    dve.bn_aggr(mv[:, norm, u, :], stats[:, norm, u, :]).then_inc(ln_step[norm], 1)
                wait_for(dve, ln_step[norm], LNS, item, 2 * U + 1)
                dve.tensor_scalar(ve[:, norm, :], mv[:, norm, :, 1], LN_EPS, None, ALU.add).then_inc(ln_var[norm], 1)
                for u, tile in enumerate(tiles):
                    dve.scalar_tensor_tensor(out=tile, in0=tile, scalar=mv[:, norm, u, 0:1],
                                             in1=vec[f"g{norm + 1}"][:, :], op0=ALU.subtract, op1=ALU.mult
                                             ).then_inc(ln_scaled[norm], 1)

            def normalise(norm, item, tiles):
                r, t, z = rs[:, norm, 0, :], rs[:, norm, 1, :], rs[:, norm, 2, :]
                wait_for(dve, ln_sd[norm], 1, item, 1)
                dve.reciprocal(r, sd[:, norm, :]).then_inc(ln_step[norm], 1)
                wait_for(dve, ln_step[norm], LNS, item, 2 * U + 2)
                dve.tensor_tensor(t, r, r, ALU.mult).then_inc(ln_step[norm], 1)
                wait_for(dve, ln_step[norm], LNS, item, 2 * U + 3)
                dve.tensor_tensor(t, t, ve[:, norm, :], ALU.mult).then_inc(ln_step[norm], 1)
                wait_for(dve, ln_step[norm], LNS, item, 2 * U + 4)
                dve.tensor_scalar(t, t, -0.5, 1.5, ALU.mult, ALU.add).then_inc(ln_step[norm], 1)
                wait_for(dve, ln_step[norm], LNS, item, 2 * U + 5)
                dve.tensor_tensor(z, r, t, ALU.mult).then_inc(ln_root[norm], 1)
                wait_for(dve, ln_root[norm], 1, item, 1)
                for u, tile in enumerate(tiles):
                    wait_for(dve, ln_scaled[norm], U, item, u + 1)
                    dve.scalar_tensor_tensor(out=tile, in0=tile, scalar=z[:, u:u + 1],
                                             in1=vec[f"be{norm + 1}"][:, :], op0=ALU.mult, op1=ALU.add
                                             ).then_inc(ln_out[norm], 1)

            dve.wait_ge(front_loaded, 16 * (len(FRONT_VECTORS) + 1))

            def emit(window):
                for s in range(SLOTS):
                    for kind, at in ((0, OTR), (1, X1_TURN)):
                        for u in range(U):
                            for item, _ in due(window, s, SLOTS, CHUNKS, at + (2 * u, u)[kind]):
                                wait_for(dve, (early.o_loaded, x1_loaded)[kind][u], 64, item, 64)
                                wait_for(dve, turned_lo, 2 * U, item, U * kind + u)
                                dve.transpose(block_turned[:, :, :].bitcast(U32),
                                              o_in[:, u, :].bitcast(U32).rearrange("p (k t) -> p k t", t=P)
                                              ).then_inc((ctx_turned, x1_turned)[kind], 1)
                    for kind, at in ((0, OTR), (1, X1_TURN)):
                        for u in range(U):
                            for item, _ in due(window, s, SLOTS, CHUNKS, at + (1 + 2 * u, u)[kind]):
                                n = U * kind + u
                                wait_for(dve, turned_hi, 2 * U, item, n + 1)
                                both = turned[:, item.parity, :, :, u * P:(u + 1) * P]
                                dve.tensor_tensor(both[:, 1, :, :], block_turned[:, :, :], both[:, 0, :, :], ALU.subtract
                                                  ).then_inc(turned_lo, 1)
                    for n in weights_due(window, s):
                        dve.wait_ge(w_hi, n + 1)
                        dst = chunks[n][1]
                        dve.tensor_tensor(dst[:, 1, :], raw[:, n % RAW, :], dst[:, 0, :], ALU.subtract
                                          ).then_inc(w_lo, 1)
                    for u in range(U):
                        for item, _ in due(window, s, SLOTS, CHUNKS, RES + 2 * u):
                            wait_for(dve, proj_done, U, item, u + 1)
                            wait_for(dve, bo_added, U, item, u + 1)
                            wait_for(dve, y_done, U, item, -U)
                            tile = x1[:, item.parity, u, :]
                            dve.tensor_tensor(tile, front[:, u, :], x_in[:, u, :], ALU.add).then_inc(res_done, 1)
                            wait_for(dve, res_done, U, item, u + 1)
                            statistics(0, item, u, tile)
                            if u == U - 1:
                                variance(0, item, [x1[:, item.parity, v, :] for v in range(U)])
                    for item, _ in due(window, s, SLOTS, CHUNKS, NORM1):
                        normalise(0, item, [x1[:, item.parity, u, :] for u in range(U)])
                    for item, _ in due(window, s, SLOTS, CHUNKS, RES2):
                        if isinstance(item.n, int) and item.n == 0:
                            dve.wait_ge(back_loaded, 16 * len(BACK_VECTORS))
                        for u in range(U):
                            wait_for(dve, ffn_done, FT, item, FT)
                            wait_for(dve, b2_added, U, item, u + 1)
                            wait_for(dve, y_stored, 16, item, 0)
                            dve.tensor_tensor(y[:, u, :], acc[:, item.parity, u, :], x1[:, item.parity, u, :],
                                              ALU.add).then_inc(y_done, 1)
                            wait_for(dve, y_done, U, item, u + 1)
                            statistics(1, item, u, y[:, u, :])
                        variance(1, item, [y[:, u, :] for u in range(U)])
                    for item, _ in due(window, s, SLOTS, CHUNKS, RES2 + 1):
                        normalise(1, item, [y[:, u, :] for u in range(U)])
                    for item, f in due(window, s, SLOTS, CHUNKS, FFN1, FT):
                        wait_for(dve, h_out, FT, item, f + 1)
                        dve.tensor_tensor(hs[:, f % 4, 1, :], hf[:, f % 2, :], hs[:, f % 4, 0, :], ALU.subtract
                                          ).then_inc(h_lo, 1)

            run_windows(dve, CHUNKS, emit, PEELED)

        @block.tensor
        def _(pe):
            def emit(window):
                for s in range(SLOTS):
                    for u in range(U):
                        for item, half in due(window, s, SLOTS, CHUNKS, PROJ + 2 * u, 2):
                            if half == 0:
                                wait_for(pe, turned_lo, 2 * U, item, u + 1)
                                wait_for(pe, res_done, U, item, u + 1 - U)
                                if isinstance(item.n, int) and item.n == 0:
                                    pe.wait_ge(w_lo, KT)
                            for j in range(half * KT // 2, (half + 1) * KT // 2):
                                for m, (aa, aw) in enumerate(((0, 0), (0, 1), (1, 0))):
                                    last = pe.matmul(front[:, u, :], turned[:, item.parity, aa, j, u * P:(u + 1) * P],
                                                     Wo[:, aw, j, :], start=(j == 0 and m == 0),
                                                     stop=(j == KT - 1 and m == 2))
                            if half:
                                last.then_inc(proj_done, 1)
                    for item, f in due(window, s, SLOTS, CHUNKS, FFN1, FT):
                        if f == 0:
                            wait_for(pe, turned_lo, 2 * U, item, 2 * U)
                        if isinstance(item.n, int) and item.n == 0:
                            pe.wait_ge(w_lo, w1_chunks(f))
                        wait_for(pe, h_out, FT, item, f + 1 - 2)
                        for j in range(KT):
                            for m, (aw, aa) in enumerate(((0, 0), (0, 1), (1, 0))):
                                last = pe.matmul(h_ps[:, f % 2, 0:T], W1[:, aw, j, f * P:(f + 1) * P],
                                                 turned[:, item.parity, aa, j, :], start=(j == 0 and m == 0),
                                                 stop=(j == KT - 1 and m == 2))
                        last.then_inc(h_done, 1)
                    for item, f in due(window, s, SLOTS, CHUNKS, FFN2, FT):
                        if f == 0:
                            wait_for(pe, y_done, U, item, -U)
                        if isinstance(item.n, int) and item.n == 0:
                            pe.wait_ge(w_lo, w2_chunks(f))
                        wait_for(pe, h_lo, FT, item, f + 1)
                        for u in range(U):
                            for m, (aa, aw) in enumerate(((0, 0), (0, 1), (1, 0))):
                                last = pe.matmul(acc[:, item.parity, u, :], hs[:, f % 4, aa, u * P:(u + 1) * P],
                                                 W2[:, aw, f, :], start=(f == 0 and m == 0),
                                                 stop=(f == FT - 1 and m == 2))
                        last.then_inc(ffn_done, 1)

            run_windows(pe, CHUNKS, emit, PEELED)


INPUTS = ["xT", "cT", "x", "Wq", "Wk", "Wv", "Wo", "W1", "W2", "bq", "bk", "bv", "b1",
          "bo", "g1", "be1", "b2", "g2", "be2"]


def build(nc, a, out):
    tokens, d = a["x"].shape
    ctx_rows = nc.dram_tensor("ctx_rows", [tokens, d], F32, kind="Internal").ap()
    vectors = {v: a[v] for v in FRONT_VECTORS + BACK_VECTORS}
    with ExitStack() as stack:
        early = Early(nc, stack, d, a["W1"].shape[1])
        all_stored = attention(nc, a["xT"], a["cT"], {w: a["W" + w] for w in "vkq"}, {w: a["b" + w] for w in "kq"},
                               a["bv"], ctx_rows, early.stored,
                               lambda sp: early.load(sp, ctx_rows, a["x"], a["Wo"], a["b1"], vectors))
        feed(nc, ctx_rows, all_stored, a["x"], a["Wo"], a["W1"], a["W2"], early, out)


def kernel(**inputs):
    import concourse.bacc as bacc
    from concourse.bass_utils import run_bass_kernel_spmd

    def given(name):
        return np.asarray(inputs[name])

    def columns(v):
        return v.reshape(-1, P).T

    x, ctx = given("x"), given("ctx_1024")
    b, s, d = x.shape
    w = {n: given("L0_xattn_" + n) for n in ("Wq", "Wk", "Wv", "Wo", "W1", "W2", "bq", "bk", "bv", "bo", "b1", "b2",
                                             "ln1_g", "ln1_b", "ln2_g", "ln2_b")}
    layout = {"xT": x.transpose(0, 2, 1), "cT": ctx.transpose(0, 2, 1), "x": x.reshape(b * s, d),
              "Wq": w["Wq"], "Wk": w["Wk"], "Wv": w["Wv"], "Wo": w["Wo"], "W1": w["W1"], "W2": w["W2"],
              "bq": columns(w["bq"]), "bk": columns(w["bk"]), "bv": w["bv"], "b1": columns(w["b1"]),
              "bo": w["bo"], "g1": w["ln1_g"], "be1": w["ln1_b"], "b2": w["b2"], "g2": w["ln2_g"], "be2": w["ln2_b"]}
    nc = bacc.Bacc("TRN2", target_bir_lowering=False, num_devices=1, dynamic_dma_scratch_size=2048)
    arrays, args = {}, {}
    for name in INPUTS:
        arrays["in_" + name] = np.ascontiguousarray(layout[name])
        args[name] = nc.dram_tensor("in_" + name, arrays["in_" + name].shape, F32, kind="ExternalInput").ap()
    out = nc.dram_tensor("out", [b * s, d], F32, kind="ExternalOutput").ap()
    build(nc, args, out)
    result = run_bass_kernel_spmd(nc, [arrays], core_ids=[0])
    return result.results[0]["out"].reshape(b, s, d)
```
